# Optimizing a Trainium2 kernel written in Bass

```python
import numpy as np
import jax
import jax.numpy as jnp

def _softmax(x, axis=-1):
    return jax.nn.softmax(x, axis=axis)

def _gelu(x):
    return jax.nn.gelu(x, approximate=True)

def _silu(x):
    return jax.nn.silu(x)

def _sigmoid(x):
    return jax.nn.sigmoid(x)

def _layernorm(x, axis=-1, eps=1e-05):
    m = jnp.mean(x, axis=axis, keepdims=True)
    v = jnp.var(x, axis=axis, keepdims=True)
    return (x - m) / jnp.sqrt(v + eps)

def _scatter_add(tgt, idx, src, axis=0):
    return tgt.at[idx].add(src)

def _segment_sum(src, seg, n):
    return jax.ops.segment_sum(src, seg, n)
kernel_name = 'mk_seq_preln_d2_jaxref_r4_179e84'

def setup_inputs(seed: int=0):
    np.random.seed(seed)
    _w = jnp.asarray

    def _L0_attn_setup():
        import jax, jax.numpy as jnp
        import numpy as np
        DIM = 512
        STATE = 64
        DT_RANK = 128
        CHUNK = 128
        key = jax.random.key(seed)
        ks = jax.random.split(key, 8)
        B, L, D, N, R = (4, 512, DIM, STATE, DT_RANK)
        x = jax.random.normal(ks[0], (B, L, D), dtype=jnp.float32)
        norm_w = jnp.ones((D,), jnp.float32)
        norm_b = jnp.zeros((D,), jnp.float32)
        x_proj_w = jax.random.normal(ks[1], (R + 2 * N, D), jnp.float32) * (1.0 / np.sqrt(D))
        dt_proj_w = jax.random.normal(ks[2], (D, R), jnp.float32) * (1.0 / np.sqrt(R))
        dt_proj_b = jax.random.normal(ks[3], (D,), jnp.float32) * 0.01
        A_log = jnp.log(jnp.tile(jnp.arange(1, N + 1, dtype=jnp.float32)[None, :], (D, 1)))
        D_param = jnp.ones((D,), jnp.float32)
        out_proj_w = jax.random.normal(ks[4], (D, D), jnp.float32) * (1.0 / np.sqrt(D))
        return {'x': x, 'norm_w': norm_w, 'norm_b': norm_b, 'x_proj_w': x_proj_w, 'dt_proj_w': dt_proj_w, 'dt_proj_b': dt_proj_b, 'A_log': A_log, 'D_param': D_param, 'out_proj_w': out_proj_w}
    _L0_attn_in = _L0_attn_setup()

    def _L0_ffn_setup():
        import jax, jax.numpy as jnp
        import numpy as np
        TOP_K = 2
        key = jax.random.key(seed)
        k1, k2, k3, k4 = jax.random.split(key, 4)
        B, S, D, E = (4, 512, 512, 8)
        x = jax.random.normal(k1, (B, S, D), dtype=jnp.float32)
        router_w = jax.random.normal(k2, (D, E), dtype=jnp.float32) * 0.02
        expert_w = jax.random.normal(k3, (E, D, D), dtype=jnp.float32) * 0.02
        expert_b = jax.random.normal(k4, (E, D), dtype=jnp.float32) * 0.02
        return {'x': x, 'router_w': router_w, 'expert_w': expert_w, 'expert_b': expert_b}
    _L0_ffn_in = _L0_ffn_setup()

    def _L1_attn_setup():
        import jax, jax.numpy as jnp
        import numpy as np
        B, T, C = (2, 512, 512)
        HS = 64
        H = C // HS
        LN_EPS = 1e-05

        def _reference_tuple_inner(x, ln_scale, ln_bias, Wx, Ww, bw, Wk, Wv, Wr, Wo):
            Bv, Tv, Cv = x.shape
            mu = jnp.mean(x, axis=-1, keepdims=True)
            var = jnp.var(x, axis=-1, keepdims=True)
            xn = (x - mu) / jnp.sqrt(var + LN_EPS) * ln_scale + ln_bias
            w_dec = jax.nn.sigmoid(xn @ Wx.T @ Ww.T + bw)
            k = xn @ Wk.T
            v = xn @ Wv.T
            r = jax.nn.sigmoid(xn @ Wr.T)
            to_tbhd = lambda a: a.reshape(Bv, Tv, H, HS).transpose(1, 0, 2, 3)
            kT, vT, wT, rT = map(to_tbhd, (k, v, w_dec, r))

            def step(state, inp):
                k_t, v_t, w_t, r_t = inp
                kv = k_t[..., :, None] * v_t[..., None, :]
                state = (1.0 - w_t)[..., :, None] * state + kv
                out = jnp.einsum('bhd,bhde->bhe', r_t, state)
                return (state, out)
            state0 = jnp.zeros((Bv, H, HS, HS), x.dtype)
            state, outs = jax.lax.scan(step, state0, (kT, vT, wT, rT))
            y = outs.transpose(1, 0, 2, 3).reshape(Bv, Tv, Cv) @ Wo.T
            return (y, state)
        key = jax.random.key(seed)
        ks = jax.random.split(key, 8)
        w = lambda k: jax.random.normal(k, (C, C), jnp.float32) * 0.02
        return {'x': jax.random.normal(ks[0], (B, T, C), jnp.float32), 'ln_scale': jnp.ones((C,), jnp.float32), 'ln_bias': jnp.zeros((C,), jnp.float32), 'Wx': w(ks[1]), 'Ww': w(ks[2]), 'bw': jnp.zeros((C,), jnp.float32), 'Wk': w(ks[3]), 'Wv': w(ks[4]), 'Wr': w(ks[5]), 'Wo': w(ks[6])}
    _L1_attn_in = _L1_attn_setup()

    def _L1_ffn_setup():
        import jax, jax.numpy as jnp
        import numpy as np
        D_MODEL = 512
        NUM_TILES = 64
        D_SLICE = D_MODEL // NUM_TILES
        TILES_PER_CLUSTER = 8
        NUM_CLUSTERS = NUM_TILES // TILES_PER_CLUSTER
        GRID = 16
        LN_EPS = 1e-05
        DIMS = (np.arange(NUM_TILES)[:, None] * D_SLICE + np.arange(D_SLICE)[None, :]) % D_MODEL
        DIMS = jnp.asarray(DIMS, dtype=jnp.int32)

        def _forward(x, ln_gamma, ln_beta, spline_bases, spline_slopes, output_scale):
            B, S, D = x.shape
            N = B * S
            mu = jnp.mean(x, axis=-1, keepdims=True)
            var = jnp.mean(jnp.square(x - mu), axis=-1, keepdims=True)
            xn = (x - mu) * jax.lax.rsqrt(var + LN_EPS) * ln_gamma + ln_beta
            xf = xn.reshape(N, D)
            slope_sign = jnp.sign(jnp.mean(spline_slopes, axis=-1))
            tile_sigs = jnp.zeros((NUM_TILES, D), dtype=x.dtype)
            tile_sigs = tile_sigs.at[jnp.arange(NUM_TILES)[:, None], DIMS].set(slope_sign)
            cluster_sigs = jnp.sign(tile_sigs.reshape(NUM_CLUSTERS, TILES_PER_CLUSTER, D).mean(axis=1))
            cluster_assign = jnp.arange(NUM_TILES, dtype=jnp.int32) // TILES_PER_CLUSTER
            input_sigs = jnp.sign(xf)
            cluster_scores = input_sigs @ cluster_sigs.T
            best_cluster = jnp.argmax(cluster_scores, axis=-1)
            tile_scores = input_sigs @ tile_sigs.T
            in_cluster = cluster_assign[None, :] == best_cluster[:, None]
            tile_idx = jnp.argmax(jnp.where(in_cluster, tile_scores, -jnp.inf), axis=-1)
            tok_dims = DIMS[tile_idx]
            x_slice = jnp.take_along_axis(xf, tok_dims, axis=1)
            tok_min = x_slice.min(axis=1)
            tok_max = x_slice.max(axis=1)
            onehot = tile_idx[None, :] == jnp.arange(NUM_TILES)[:, None]
            tile_min = jnp.where(onehot, tok_min[None, :], jnp.inf).min(axis=1)
            tile_max = jnp.where(onehot, tok_max[None, :], -jnp.inf).max(axis=1)
            mn = tile_min[tile_idx][:, None]
            mx = tile_max[tile_idx][:, None]
            u = jnp.clip((x_slice - mn) / (mx - mn + 1e-08), 0.0, 1.0 - 1e-06)
            gi = jnp.clip((u * GRID).astype(jnp.int32), 0, GRID - 1)
            j = jnp.arange(D_SLICE)[None, :]
            b = spline_bases[tile_idx[:, None], j, gi]
            s = spline_slopes[tile_idx[:, None], j, gi]
            x_local = (u - gi.astype(u.dtype) / GRID) * GRID
            delta = (b + s * x_local) * output_scale[tile_idx][:, None]
            out = jnp.zeros_like(xf).at[jnp.arange(N)[:, None], tok_dims].set(delta)
            return x + out.reshape(B, S, D)
        key = jax.random.key(seed)
        k1, k2, k3, k4, k5, k6 = jax.random.split(key, 6)
        x = jax.random.normal(k1, (4, 1024, D_MODEL), dtype=jnp.float32)
        ln_gamma = 1.0 + 0.1 * jax.random.normal(k2, (D_MODEL,), dtype=jnp.float32)
        ln_beta = 0.1 * jax.random.normal(k3, (D_MODEL,), dtype=jnp.float32)
        spline_bases = 0.1 * jax.random.normal(k4, (NUM_TILES, D_SLICE, GRID), dtype=jnp.float32)
        spline_slopes = 0.1 + 0.1 * jax.random.normal(k5, (NUM_TILES, D_SLICE, GRID), dtype=jnp.float32)
        output_scale = 1.0 + 0.1 * jax.random.normal(k6, (NUM_TILES,), dtype=jnp.float32)
        return {'x': x, 'ln_gamma': ln_gamma, 'ln_beta': ln_beta, 'spline_bases': spline_bases, 'spline_slopes': spline_slopes, 'output_scale': output_scale}
    _L1_ffn_in = _L1_ffn_setup()
    _d = {'L0_attn_x': _L0_attn_in['x'], 'L0_attn_norm_w': _L0_attn_in['norm_w'], 'L0_attn_norm_b': _L0_attn_in['norm_b'], 'L0_attn_x_proj_w': _L0_attn_in['x_proj_w'], 'L0_attn_dt_proj_w': _L0_attn_in['dt_proj_w'], 'L0_attn_dt_proj_b': _L0_attn_in['dt_proj_b'], 'L0_attn_A_log': _L0_attn_in['A_log'], 'L0_attn_D_param': _L0_attn_in['D_param'], 'L0_attn_out_proj_w': _L0_attn_in['out_proj_w'], 'L0_ffn_router_w': _L0_ffn_in['router_w'], 'L0_ffn_expert_w': _L0_ffn_in['expert_w'], 'L0_ffn_expert_b': _L0_ffn_in['expert_b'], 'L1_attn_ln_scale': _L1_attn_in['ln_scale'], 'L1_attn_ln_bias': _L1_attn_in['ln_bias'], 'L1_attn_Wx': _L1_attn_in['Wx'], 'L1_attn_Ww': _L1_attn_in['Ww'], 'L1_attn_bw': _L1_attn_in['bw'], 'L1_attn_Wk': _L1_attn_in['Wk'], 'L1_attn_Wv': _L1_attn_in['Wv'], 'L1_attn_Wr': _L1_attn_in['Wr'], 'L1_attn_Wo': _L1_attn_in['Wo'], 'L1_ffn_ln_gamma': _L1_ffn_in['ln_gamma'], 'L1_ffn_ln_beta': _L1_ffn_in['ln_beta'], 'L1_ffn_spline_bases': _L1_ffn_in['spline_bases'], 'L1_ffn_spline_slopes': _L1_ffn_in['spline_slopes'], 'L1_ffn_output_scale': _L1_ffn_in['output_scale']}
    _x0 = _d['L0_attn_x']
    _d['L0_attn_x'] = jax.random.normal(jax.random.fold_in(jax.random.key(seed), 1), (2, 4096, 512), dtype=_x0.dtype)
    del _x0
    return _d

def reference(L0_attn_x, L0_attn_norm_w, L0_attn_norm_b, L0_attn_x_proj_w, L0_attn_dt_proj_w, L0_attn_dt_proj_b, L0_attn_A_log, L0_attn_D_param, L0_attn_out_proj_w, L0_ffn_router_w, L0_ffn_expert_w, L0_ffn_expert_b, L1_attn_ln_scale, L1_attn_ln_bias, L1_attn_Wx, L1_attn_Ww, L1_attn_bw, L1_attn_Wk, L1_attn_Wv, L1_attn_Wr, L1_attn_Wo, L1_ffn_ln_gamma, L1_ffn_ln_beta, L1_ffn_spline_bases, L1_ffn_spline_slopes, L1_ffn_output_scale):

    def _L0_attn_ref(x, norm_w, norm_b, x_proj_w, dt_proj_w, dt_proj_b, A_log, D_param, out_proj_w):
        import jax, jax.numpy as jnp
        import numpy as np
        DIM = 512
        STATE = 64
        DT_RANK = 128
        CHUNK = 128
        B, L, D = x.shape
        N = STATE
        mu = jnp.mean(x, axis=-1, keepdims=True)
        var = jnp.var(x, axis=-1, keepdims=True)
        xn = (x - mu) / jnp.sqrt(var + 1e-05) * norm_w + norm_b
        proj = xn @ x_proj_w.T
        R = dt_proj_w.shape[1]
        delta, B_ssm, C_ssm = jnp.split(proj, [R, R + N], axis=-1)
        delta = jax.nn.softplus(delta @ dt_proj_w.T + dt_proj_b)
        A = -jnp.exp(A_log)
        c_idx = jnp.arange(L) % CHUNK
        C_used = C_ssm[:, c_idx, :]

        def step(h, inp):
            dt, b, xt, c = inp
            dA = jnp.exp(dt[:, :, None] * A)
            h = dA * h + dt[:, :, None] * b[:, None, :] * xt[:, :, None]
            y = jnp.einsum('bdn,bn->bd', h, c)
            return (h, y)
        h0 = jnp.zeros((B, D, N), x.dtype)
        xs = (jnp.moveaxis(delta, 1, 0), jnp.moveaxis(B_ssm, 1, 0), jnp.moveaxis(xn, 1, 0), jnp.moveaxis(C_used, 1, 0))
        _, ys = jax.lax.scan(step, h0, xs)
        y = jnp.moveaxis(ys, 0, 1)
        return (y + x * D_param) @ out_proj_w.T

    def _L0_ffn_ref(x, router_w, expert_w, expert_b):
        import jax, jax.numpy as jnp
        import numpy as np
        TOP_K = 2
        router_logits = jnp.einsum('bsd,de->bse', x, router_w)
        routing_weights = jax.nn.softmax(router_logits, axis=-1)
        weights, selected_experts = jax.lax.top_k(routing_weights, TOP_K)
        weights = weights / jnp.sum(weights, axis=-1, keepdims=True)
        _ = (weights, selected_experts)
        out = jnp.einsum('bsd,od->bso', x, expert_w[0]) + expert_b[0]
        return out

    def _L1_attn_ref(x, ln_scale, ln_bias, Wx, Ww, bw, Wk, Wv, Wr, Wo):
        import jax, jax.numpy as jnp
        import numpy as np
        B, T, C = (2, 512, 512)
        HS = 64
        H = C // HS
        LN_EPS = 1e-05

        def _reference_tuple_inner(x, ln_scale, ln_bias, Wx, Ww, bw, Wk, Wv, Wr, Wo):
            Bv, Tv, Cv = x.shape
            mu = jnp.mean(x, axis=-1, keepdims=True)
            var = jnp.var(x, axis=-1, keepdims=True)
            xn = (x - mu) / jnp.sqrt(var + LN_EPS) * ln_scale + ln_bias
            w_dec = jax.nn.sigmoid(xn @ Wx.T @ Ww.T + bw)
            k = xn @ Wk.T
            v = xn @ Wv.T
            r = jax.nn.sigmoid(xn @ Wr.T)
            to_tbhd = lambda a: a.reshape(Bv, Tv, H, HS).transpose(1, 0, 2, 3)
            kT, vT, wT, rT = map(to_tbhd, (k, v, w_dec, r))

            def step(state, inp):
                k_t, v_t, w_t, r_t = inp
                kv = k_t[..., :, None] * v_t[..., None, :]
                state = (1.0 - w_t)[..., :, None] * state + kv
                out = jnp.einsum('bhd,bhde->bhe', r_t, state)
                return (state, out)
            state0 = jnp.zeros((Bv, H, HS, HS), x.dtype)
            state, outs = jax.lax.scan(step, state0, (kT, vT, wT, rT))
            y = outs.transpose(1, 0, 2, 3).reshape(Bv, Tv, Cv) @ Wo.T
            return (y, state)
        return _reference_tuple_inner(x, ln_scale, ln_bias, Wx, Ww, bw, Wk, Wv, Wr, Wo)[0]

    def _L1_ffn_ref(x, ln_gamma, ln_beta, spline_bases, spline_slopes, output_scale):
        import jax, jax.numpy as jnp
        import numpy as np
        D_MODEL = 512
        NUM_TILES = 64
        D_SLICE = D_MODEL // NUM_TILES
        TILES_PER_CLUSTER = 8
        NUM_CLUSTERS = NUM_TILES // TILES_PER_CLUSTER
        GRID = 16
        LN_EPS = 1e-05
        DIMS = (np.arange(NUM_TILES)[:, None] * D_SLICE + np.arange(D_SLICE)[None, :]) % D_MODEL
        DIMS = jnp.asarray(DIMS, dtype=jnp.int32)

        def _forward(x, ln_gamma, ln_beta, spline_bases, spline_slopes, output_scale):
            B, S, D = x.shape
            N = B * S
            mu = jnp.mean(x, axis=-1, keepdims=True)
            var = jnp.mean(jnp.square(x - mu), axis=-1, keepdims=True)
            xn = (x - mu) * jax.lax.rsqrt(var + LN_EPS) * ln_gamma + ln_beta
            xf = xn.reshape(N, D)
            slope_sign = jnp.sign(jnp.mean(spline_slopes, axis=-1))
            tile_sigs = jnp.zeros((NUM_TILES, D), dtype=x.dtype)
            tile_sigs = tile_sigs.at[jnp.arange(NUM_TILES)[:, None], DIMS].set(slope_sign)
            cluster_sigs = jnp.sign(tile_sigs.reshape(NUM_CLUSTERS, TILES_PER_CLUSTER, D).mean(axis=1))
            cluster_assign = jnp.arange(NUM_TILES, dtype=jnp.int32) // TILES_PER_CLUSTER
            input_sigs = jnp.sign(xf)
            cluster_scores = input_sigs @ cluster_sigs.T
            best_cluster = jnp.argmax(cluster_scores, axis=-1)
            tile_scores = input_sigs @ tile_sigs.T
            in_cluster = cluster_assign[None, :] == best_cluster[:, None]
            tile_idx = jnp.argmax(jnp.where(in_cluster, tile_scores, -jnp.inf), axis=-1)
            tok_dims = DIMS[tile_idx]
            x_slice = jnp.take_along_axis(xf, tok_dims, axis=1)
            tok_min = x_slice.min(axis=1)
            tok_max = x_slice.max(axis=1)
            onehot = tile_idx[None, :] == jnp.arange(NUM_TILES)[:, None]
            tile_min = jnp.where(onehot, tok_min[None, :], jnp.inf).min(axis=1)
            tile_max = jnp.where(onehot, tok_max[None, :], -jnp.inf).max(axis=1)
            mn = tile_min[tile_idx][:, None]
            mx = tile_max[tile_idx][:, None]
            u = jnp.clip((x_slice - mn) / (mx - mn + 1e-08), 0.0, 1.0 - 1e-06)
            gi = jnp.clip((u * GRID).astype(jnp.int32), 0, GRID - 1)
            j = jnp.arange(D_SLICE)[None, :]
            b = spline_bases[tile_idx[:, None], j, gi]
            s = spline_slopes[tile_idx[:, None], j, gi]
            x_local = (u - gi.astype(u.dtype) / GRID) * GRID
            delta = (b + s * x_local) * output_scale[tile_idx][:, None]
            out = jnp.zeros_like(xf).at[jnp.arange(N)[:, None], tok_dims].set(delta)
            return x + out.reshape(B, S, D)
        return _forward(x, ln_gamma, ln_beta, spline_bases, spline_slopes, output_scale)
    x = L0_attn_x
    x = x + _L0_attn_ref(_layernorm(x, axis=-1), L0_attn_norm_w, L0_attn_norm_b, L0_attn_x_proj_w, L0_attn_dt_proj_w, L0_attn_dt_proj_b, L0_attn_A_log, L0_attn_D_param, L0_attn_out_proj_w)
    x = x + _L0_ffn_ref(_layernorm(x, axis=-1), L0_ffn_router_w, L0_ffn_expert_w, L0_ffn_expert_b)
    x = x + _L1_attn_ref(_layernorm(x, axis=-1), L1_attn_ln_scale, L1_attn_ln_bias, L1_attn_Wx, L1_attn_Ww, L1_attn_bw, L1_attn_Wk, L1_attn_Wv, L1_attn_Wr, L1_attn_Wo)
    x = x + _L1_ffn_ref(_layernorm(x, axis=-1), L1_ffn_ln_gamma, L1_ffn_ln_beta, L1_ffn_spline_bases, L1_ffn_spline_slopes, L1_ffn_output_scale)
    return x

_drawn_inputs = setup_inputs


def setup_inputs(seed=0):
    import zlib

    import numpy as np

    out = dict(_drawn_inputs(seed))
    spreads = {'L0_attn_norm_w': (1.0, 0.2),
     'L0_attn_norm_b': (0.0, 0.1),
     'L0_attn_D_param': (1.0, 0.584),
     'L1_attn_ln_scale': (1.0, 0.6),
     'L1_attn_ln_bias': (0.0, 0.8),
     'L1_attn_bw': (0.0, 0.8)}
    factors = {'L0_attn_dt_proj_b': 8.0,
     'L0_ffn_expert_b': 8.0,
     'L1_attn_Wx': 8.0,
     'L1_attn_Ww': 8.0,
     'L1_attn_Wr': 4.276,
     'L1_ffn_ln_gamma': 8.0,
     'L1_ffn_ln_beta': 8.0,
     'L1_ffn_spline_bases': 8.0,
     'L1_ffn_spline_slopes': 8.0,
     'L1_ffn_output_scale': 37.702}
    for name, (base, spread) in spreads.items():
        noise = np.random.default_rng([zlib.crc32(name.encode()), seed]).standard_normal(out[name].shape)
        drawn = base * np.exp(spread * noise) if base else spread * noise
        out[name] = jnp.asarray(drawn.astype(out[name].dtype))
    for name, factor in factors.items():
        out[name] = (out[name] * factor).astype(out[name].dtype)
    return out
```

```python
from contextlib import ExitStack
import concourse.bass as bass
from concourse import mybir
ALU = mybir.AluOpType
ACT = mybir.ActivationFunctionType
AX = mybir.AxisListType
F32 = mybir.dt.float32
P = 128
T = 512
EPS = 1e-5
HEADS = 8


class Count:

    def __init__(self, sem, per):
        self.sem, self.per, self.n, self.item = sem, per, 0, 0

    def start(self, eng):
        eng.sem_inc(self.sem, 2 * self.per)

    def begin(self, item):
        assert self.n in (0, self.per), (self.sem, self.n)
        self.item, self.n = item, 0

    def inc(self, ins):
        self.n += 1
        assert self.n <= self.per, self.sem
        ins.then_inc(self.sem, 1)
        return self.n

    def link(self, eng, ins):
        self.inc(ins)
        eng.wait_ge(self.sem, (self.item + 2) * self.per + self.n)

    def wait(self, eng, item, n):
        eng.wait_ge(self.sem, (item + 2) * self.per + n)

    def wait_freed(self, eng, item):
        eng.wait_ge(self.sem, (item + 1) * self.per)

    def wait_before(self, eng, item):
        eng.wait_ge(self.sem, (item + 2) * self.per)

    def wait_all(self, eng, item):
        eng.wait_ge(self.sem, (item + 3) * self.per)


def skewed(eng, items, pieces):

    def turn(m, par, ahead=True, behind=True):
        for lead, piece in pieces:
            if lead and ahead:
                piece(m * 2 + par + 1, 1 - par, m + par)
            if not lead and behind:
                piece(m * 2 + par, par, m)

    for lead, piece in pieces:
        if lead:
            piece(0, 0, 0)
    if items > 2:
        with eng.Fori(0, items // 2 - 1) as m:
            turn(m, 0)
            turn(m, 1)
    turn(items // 2 - 1, 0)
    turn(items // 2 - 1, 1, ahead=False)


def staggered(eng, items, pieces):

    def turn(m, par, most=2):
        for lead, piece in pieces:
            if lead <= most:
                piece(m * 2 + par + lead, (par + lead) % 2, m + (par + lead) // 2)

    for before in (2, 1):
        for lead, piece in pieces:
            if lead >= before:
                piece(lead - before, (lead - before) % 2, 0)
    if items > 2:
        with eng.Fori(0, items // 2 - 1) as m:
            turn(m, 0)
            turn(m, 1)
    turn(items // 2 - 1, 0, 1)
    turn(items // 2 - 1, 1, 0)


def in_turn(eng, items, only):
    with eng.Fori(0, items // 2) as m:
        for par in range(2):
            only(m * 2 + par, par, m)


NORM_DVE = 8
NORM_VE = 3


def hold(eng, ticks):
    eng.sem_inc(ticks, 1)


def norm_dve(dve, ticks, cnt, roots, item, root_n, out, x, st, mv, ve, r0, rr, tmp, tiles):
    for j in range(tiles):
        last = dve.bn_stats(st[:, j, :], x[:, j, :])
    cnt.link(dve, last)
    hold(dve, ticks)
    for j in range(tiles):
        last = dve.bn_aggr(mv[:, j, :], st[:, j, :])
    cnt.link(dve, last)
    cnt.inc(dve.tensor_scalar(ve, mv[:, :, 1], EPS, None, ALU.add))
    roots.wait(dve, item, root_n)
    cnt.link(dve, dve.tensor_tensor(tmp, r0, r0, ALU.mult))
    cnt.link(dve, dve.tensor_tensor(tmp, tmp, ve, ALU.mult))
    cnt.link(dve, dve.tensor_scalar(tmp, tmp, -0.5, 1.5, ALU.mult, ALU.add))
    cnt.link(dve, dve.tensor_tensor(rr, r0, tmp, ALU.mult))
    for j in range(tiles):
        last = dve.tensor_scalar(out[:, j, :], x[:, j, :], mv[:, j, 0:1], rr[:, j:j + 1], ALU.subtract, ALU.mult)
    cnt.link(dve, last)


def root_pool(pool, cnt, stats, item, stats_n, r0, ve, neg_half):
    stats.wait(pool, item, stats_n)
    cnt.inc(pool.tensor_tensor(r0, ve, neg_half, ALU.pow))


def pre_phase(nc, NCH, D, x_d, xp_d, dtw_d, nw_d, nb_d, dtb_d, ident_d, dt_s, v_s, z_s, bc_s):
    Q = D // P
    J = T // P
    with ExitStack() as ctx:
        sb = lambda n, s: ctx.enter_context(nc.sbuf_tensor("pre_" + n, s, F32))
        ps = lambda n, s: ctx.enter_context(nc.psum_tensor("pre_" + n, s, F32))
        sem = lambda n: ctx.enter_context(nc.semaphore("pre_" + n))
        tp = ps("tp", [P, 2, Q, T])
        x = sb("x", [P, 2, J, D]); z = sb("z", [P, 2, J, D]); zh = sb("zh", [P, 2, J, D])
        zt = sb("zt", [P, 2, Q, T]); znt = sb("znt", [P, 2, Q, T])
        dl = sb("dl", [P, T]); bc = sb("bc", [P, 2, T])
        xb = sb("xb", [P, 2, Q, T]); ab = sb("ab", [P, 2, Q, T]); dt = sb("dt", [P, 2, Q, T]); v = sb("v", [P, 2, Q, T])
        st = sb("st", [P, J, 6]); mv = sb("mv", [P, J, 2]); ve = sb("ve", [P, J])
        half_neg = sb("half_neg", [P, J]); r0 = sb("r0", [P, J]); rr = sb("rr", [P, J]); tmp = sb("tmp", [P, J])
        xp = sb("xp", [P, Q, 2 * P]); dtw = sb("dtw", [P, D]); ident = sb("ident", [P, P])
        nw = sb("nw", [P, Q]); nb = sb("nb", [P, Q]); dtb = sb("dtb", [P, Q])
        consts = sem("consts"); ticks_dve = sem("ticks_dve"); half_ready = sem("half_ready")
        x_in = [sem(f"x_in{i}") for i in range(2)]
        outs = [sem(f"outs{i}") for i in range(2)]
        norm_steps = Count(sem("norm_steps"), 2 * NORM_DVE)
        root_steps = Count(sem("root_steps"), 2)
        proj_steps = Count(sem("proj_steps"), Q + 4)
        pe_steps = Count(sem("pe_steps"), 4 + Q)
        act_steps = Count(sem("act_steps"), 2 * Q + 3)
        xv = x_d.rearrange("(c j p) d -> c p j d", j=J, p=P)
        block = ctx.enter_context(nc.Block())

        @block.sync
        def _(sp):
            for dst, src in ((xp, xp_d), (dtw, dtw_d), (ident, ident_d), (nw, nw_d), (nb, nb_d), (dtb, dtb_d)):
                sp.dma_start(dst[:], src).then_inc(consts, 16)

            for par in range(2):
                sp.sem_inc(outs[par], 64)

            def load(c, par, half):
                norm_steps.wait_freed(sp, c)
                sp.dma_start(x[:, par], xv[c]).then_inc(x_in[par], 16)

            def store(c, par, half):
                proj_steps.wait(sp, c, Q + 2)
                sp.dma_start(z_s[c], zt[:, par]).then_inc(outs[par], 16)
                sp.dma_start(bc_s[c], bc[:, par]).then_inc(outs[par], 16)
                proj_steps.wait(sp, c, Q + 3)
                sp.dma_start(dt_s[c], dt[:, par]).then_inc(outs[par], 16)
                proj_steps.wait_all(sp, c)
                sp.dma_start(v_s[c], v[:, par]).then_inc(outs[par], 16)
            skewed(sp, NCH, [(1, load), (0, store)])
            for par in range(2):
                sp.wait_ge(outs[par], 64 * (NCH // 2 + 1))

        @block.gpsimd
        def _(pool):
            root_steps.start(pool)
            pool.memset(half_neg[:], -0.5).then_inc(half_ready, 1)
            pool.wait_ge(half_ready, 1)

            def roots(c, par, half):
                root_steps.begin(c)
                root_pool(pool, root_steps, norm_steps, c, NORM_VE, r0[:], ve[:], half_neg[:])
                root_pool(pool, root_steps, norm_steps, c, NORM_DVE + NORM_VE, r0[:], ve[:], half_neg[:])
            in_turn(pool, NCH, roots)

        @block.vector
        def _(dve):
            norm_steps.start(dve)
            proj_steps.start(dve)

            def norms(c, par, half):
                norm_steps.begin(c)
                dve.wait_ge(x_in[par], (half + 1) * 16)
                pe_steps.wait_freed(dve, c)
                norm_dve(dve, ticks_dve, norm_steps, root_steps, c, 1, z[:, par], x[:, par], st, mv, ve[:], r0[:], rr[:], tmp[:], J)
                norm_dve(dve, ticks_dve, norm_steps, root_steps, c, 2, zh[:, par], z[:, par], st, mv, ve[:], r0[:], rr[:], tmp[:], J)

            def proj(c, par, half):
                proj_steps.begin(c)
                dve.wait_ge(outs[par], (half + 1) * 64)
                pe_steps.wait(dve, c, 2)
                for q in range(Q):
                    proj_steps.inc(dve.tensor_copy(zt[:, par, q, :], tp[:, par, q, :]))
                pe_steps.wait(dve, c, 3)
                proj_steps.inc(dve.tensor_copy(dl[:], tp[:, par, 0, :]))
                pe_steps.wait(dve, c, 4)
                proj_steps.inc(dve.tensor_copy(bc[:, par, :], tp[:, par, 1, :]))
                act_steps.wait_all(dve, c)
                proj_steps.link(dve, dve.scalar_tensor_tensor(out=dt[:, par], in0=xb[:, par], scalar=0.0, in1=ab[:, par], op0=ALU.max, op1=ALU.add))
                proj_steps.inc(dve.tensor_tensor(v[:, par], dt[:, par], znt[:, par], ALU.mult))
            skewed(dve, NCH, [(1, norms), (0, proj)])

        @block.scalar
        def _(act):
            act_steps.start(act)
            act.wait_ge(consts, 96)

            def evac(c, par, half):
                act_steps.begin(c)
                proj_steps.wait_freed(act, c)
                pe_steps.wait(act, c, 1)
                for q in range(Q):
                    act_steps.inc(act.activation(znt[:, par, q, :], tp[:, par, q, :], ACT.Identity, bias=nb[:, q:q + 1], scale=nw[:, q:q + 1]))
                for q in range(Q):
                    pe_steps.wait(act, c, 5 + q)
                    act_steps.inc(act.activation(xb[:, par, q, :], tp[:, par, q, :], ACT.Identity, bias=dtb[:, q:q + 1]))
                act_steps.wait(act, c, 2 * Q)
                act_steps.link(act, act.activation(ab[:, par], xb[:, par], ACT.Abs))
                act_steps.link(act, act.activation(ab[:, par], ab[:, par], ACT.Exp, scale=-1.0))
                act_steps.inc(act.activation(ab[:, par], ab[:, par], ACT.Ln, bias=1.0))
            in_turn(act, NCH, evac)

        @block.tensor
        def _(pe):
            pe_steps.start(pe)
            pe.wait_ge(consts, 96)

            def work(c, par, half):
                pe_steps.begin(c)
                norm_steps.wait_all(pe, c)
                act_steps.wait_freed(pe, c)

                def turn(src):
                    for q in range(Q):
                        for j in range(J):
                            mm = pe.transpose(tp[:, par, q, j * P:(j + 1) * P], src[:, par, j, q * P:(q + 1) * P], ident[:])
                    pe_steps.inc(mm)
                proj_steps.wait_freed(pe, c)
                turn(zh)
                act_steps.wait(pe, c, Q)
                turn(z)
                proj_steps.wait(pe, c, Q)
                for i in range(2):
                    for q in range(Q):
                        mm = pe.matmul(tp[:, par, i, :], xp[:, q, i * P:(i + 1) * P], znt[:, par, q, :], start=(q == 0), stop=(q == Q - 1))
                    pe_steps.inc(mm)
                proj_steps.wait(pe, c, Q + 2)
                for q in range(Q):
                    pe_steps.inc(pe.matmul(tp[:, par, q, :], dtw[:, q * P:(q + 1) * P], dl[:], start=True, stop=True))
            in_turn(pe, NCH, work)


def scan_phase(nc, B, L, a_log, d_diag, ident_d, dt_s, v_s, z_s, bc_s, y_s):
    NS = a_log.shape[2]
    Q = a_log.shape[1]
    KC = L // T
    NCH = B * KC
    A_SLOTS = 3
    A0 = 2 * Q
    with ExitStack() as ctx:
        sb = lambda n, s: ctx.enter_context(nc.sbuf_tensor("scan_" + n, s, F32))
        ps = lambda n, s: ctx.enter_context(nc.psum_tensor("scan_" + n, s, F32))
        sem = lambda n: ctx.enter_context(nc.semaphore("scan_" + n))
        y_ps = ps("y", [P, Q, T])
        a_ps = ps("a", [P, A_SLOTS, T])
        bb_ps = ps("bb", [P, T])
        dt = sb("dt", [P, 2, Q, T]); v = sb("v", [P, 2, Q, T]); z = sb("z", [P, 2, Q, T])
        bt = sb("bt", [P, 2, T]); bm = sb("bm", [P, 2, T])
        u = sb("u", [P, 2, Q, T]); h = sb("h", [P, 2, Q, T]); hc = sb("hc", [P, 2, Q, T])
        cb = sb("cb", [P, NS, P]); yo = sb("yo", [P, 2, Q, T])
        carry = sb("carry", [P, NS, Q])
        alog = sb("alog", [P, Q, NS]); aexp = sb("aexp", [P, Q, NS]); aneg = sb("aneg", [P, Q, NS])
        ident = sb("ident", [P, P]); ones = sb("ones", [P, P]); dd = sb("dd", [P, Q, P]); dcol = sb("dcol", [P, Q])
        consts = sem("consts"); aneg_ready = sem("aneg_ready"); ones_ready = sem("ones_ready"); dd_ready = sem("dd_ready")
        zero_ready = sem("zero_ready"); y_zeroed = sem("y_zeroed")
        ticks = {e: sem("ticks_" + e) for e in ("pool", "dve", "act")}
        dt_in, v_in, z_in, bt_in, y_out = ([sem(f"{n}{i}") for i in range(2)] for n in ("dt_in", "v_in", "z_in", "bt_in", "y_out"))
        cb_in = sem("cb_in"); cb_free = sem("cb_free")
        dt_free = sem("dt_free"); v_free = sem("v_free"); z_free = sem("z_free")
        bm_ready = sem("bm_ready")
        bb_ready = sem("bb_ready")
        a_ready = sem("a_ready")
        u_ready = sem("u_ready")
        h_ready = sem("h_ready")
        hc_ready = sem("hc_ready")
        hc_used = sem("hc_used")
        carry_saved = sem("carry_saved")
        carry_zeroed = sem("carry_zeroed")
        y_copied = sem("y_copied")
        block = ctx.enter_context(nc.Block())

        @block.sync
        def _(sp):
            for dst, src in ((alog, a_log), (ident, ident_d), (dcol, d_diag)):
                sp.dma_start(dst[:], src).then_inc(consts, 16)
            with sp.Fori(0, NCH // 2) as k:
                for par in range(2):
                    c = k * 2 + par
                    sp.wait_ge(dt_free, c + 1)
                    sp.dma_start(bt[:, par, :], bc_s[c]).then_inc(bt_in[par], 16)
                    sp.dma_start(dt[:, par], dt_s[c]).then_inc(dt_in[par], 16)
                    sp.wait_ge(v_free, c + 1)
                    sp.dma_start(v[:, par], v_s[c]).then_inc(v_in[par], 16)
                    sp.wait_ge(z_free, c + 1)
                    sp.dma_start(z[:, par], z_s[c]).then_inc(z_in[par], 16)

        @block.gpsimd
        def _(pool):
            pool.sem_inc(hc_ready, 2)
            pool.sem_inc(carry_saved, 1)
            pool.sem_inc(cb_free, 1)
            with pool.Fori(0, B) as b:
                pool.wait_ge(cb_in, (b + 1) * 16)
                hold(pool, ticks["pool"])
                with pool.Fori(0, KC) as k:
                    with pool.Fori(0, NS // 2) as m:
                        for i in range(2):
                            n = m * 2 + i
                            g = (b * KC + k) * NS + n
                            pool.wait_ge(h_ready, g * Q + Q + A0)
                            pool.tensor_copy(carry[:, bass.ds(n, 1), :].rearrange("p o q -> p (o q)"), h[:, i, :, T - 1]).then_inc(carry_saved, 1)
                            pool.wait_ge(hc_used, g + 1)
                            pool.tensor_tensor(
                                hc[:, i].rearrange("p q (r j) -> p (q r) j", j=P),
                                h[:, i].rearrange("p q (r j) -> p (q r) j", j=P),
                                cb[:, bass.ds(n, 1), :].broadcast_to([P, Q * T // P, P]), ALU.mult
                            ).then_inc(hc_ready, 1)
                pool.wait_ge(hc_ready, (b + 1) * (KC * NS) + 2)
                pool.sem_inc(cb_free, 1)

        @block.scalar
        def _(act):
            act.sem_inc(dt_free, 2)
            for par in range(2):
                act.sem_inc(y_out[par], 16)
            act.wait_ge(consts, 48)
            act.activation(aexp[:], alog[:], ACT.Exp).then_inc(aneg_ready, 1)
            act.wait_ge(aneg_ready, 1)
            act.mul(aneg[:], aexp[:], -1.0).then_inc(aneg_ready, 1)
            act.wait_ge(aneg_ready, 2)
            with act.Fori(0, B) as b:
                act.wait_ge(cb_free, b + 1)
                hold(act, ticks["act"])
                act.dma_start(cb[:], bc_s[b * KC, P // 2:P // 2 + NS, 0:P].partition_broadcast(P)).then_inc(cb_in, 16)
                with act.Fori(0, KC // 2) as k:
                    for par in range(2):
                        p = b * (KC // 2) + k
                        c = p * 2 + par

                        def mask_row(n, i):
                            act.wait_ge(bb_ready, c * NS + n + 1)
                            act.activation(bm[:, i, :], bt[:, par, :], ACT.Identity, scale=ident[:, bass.ds(n, 1)]).then_inc(bm_ready, 1)

                        def decay(n, q):
                            g = c * NS + n
                            if q == 0 or q == A_SLOTS:
                                act.wait_ge(h_ready, g * Q + A0 + (1 if q else 0))
                            act.activation(a_ps[:, q % A_SLOTS, :], dt[:, par, q, :], ACT.Exp, scale=aneg[:, q, bass.ds(n, 1)]).then_inc(a_ready, 1)

                        def step(n, ahead):
                            for q in range(A_SLOTS):
                                decay(n, q)
                            if ahead is not None:
                                mask_row(*ahead)
                            for q in range(A_SLOTS, Q):
                                decay(n, q)

                        act.wait_ge(bt_in[par], (p + 1) * 16)
                        act.wait_ge(dt_in[par], (p + 1) * 16)
                        mask_row(0, 0)
                        mask_row(1, 1)
                        step(0, (2, 0))
                        step(1, (3, 1))
                        act.wait_ge(hc_used, c * NS + 2)
                        act.wait_ge(y_zeroed, Q)
                        act.wait_ge(y_out[par], (p + 1) * 16)
                        for q in range(Q):
                            act.copy(yo[:, par, q, :], y_ps[:, q, :]).then_inc(y_copied, 1)
                        act.wait_ge(y_copied, c * Q + Q)
                        act.dma_start(y_s[c], yo[:, par]).then_inc(y_out[par], 16)
                        with act.Fori(1, NS // 2 - 1) as m:
                            for i in range(2):
                                step(m * 2 + i, (m * 2 + 2 + i, i))
                        step(NS - 2, None)
                        step(NS - 1, None)
                        act.wait_ge(a_ready, (c + 1) * NS * Q)
                        act.sem_inc(dt_free, 1)
            act.wait_ge(hc_used, NCH * NS + 2)
            act.wait_ge(y_out[0], 16 * (NCH // 2 + 1))
            for q in range(Q):
                act.copy(yo[:, 0, q, :], y_ps[:, q, :]).then_inc(y_copied, 1)
            act.wait_ge(y_copied, NCH * Q + Q)
            act.dma_start(y_s[NCH], yo[:, 0]).then_inc(y_out[0], 16)
            act.wait_ge(y_out[0], 16 * (NCH // 2 + 2))
            act.wait_ge(y_out[1], 16 * (NCH // 2 + 1))

        @block.tensor
        def _(pe):
            pe.sem_inc(bb_ready, 2)
            pe.sem_inc(hc_used, 2)
            pe.sem_inc(z_free, 2)
            pe.wait_ge(ones_ready, 1)
            pe.wait_ge(dd_ready, Q)
            pe.wait_ge(zero_ready, 1)
            for q in range(Q):
                pe.matmul(y_ps[:, q, :], ones[:], u[:, 0, q, :], start=True, stop=True).then_inc(y_zeroed, 1)
            with pe.Fori(0, NCH // 2) as p:
                for par in range(2):
                    c = p * 2 + par

                    def spread(n, i):
                        g = c * NS + n
                        pe.wait_ge(bm_ready, g + 1)
                        pe.wait_ge(u_ready, g + 2)
                        pe.matmul(bb_ps[:], ones[:], bm[:, i, :], start=True, stop=True).then_inc(bb_ready, 1)

                    def reduce(n, i, last=False):
                        pe.wait_ge(hc_ready, c * NS + n + 3)
                        for q in range(Q):
                            mm = pe.matmul(y_ps[:, q, :], ident[:], hc[:, i, q, :], start=False, stop=last)
                        mm.then_inc(hc_used, 1)

                    for n in range(3):
                        spread(n, n % 2)
                    pe.wait_ge(z_in[par], (p + 1) * 16)
                    pe.wait_ge(y_copied, c * Q + Q)
                    for q in range(Q):
                        mm = pe.matmul(y_ps[:, q, :], dd[:, q, :], z[:, par, q, :], start=True, stop=False)
                    mm.then_inc(z_free, 1)
                    with pe.Fori(0, (NS - 4) // 2) as m:
                        for i in range(2):
                            spread(m * 2 + 3 + i, (1 + i) % 2)
                            reduce(m * 2 + i, i)
                    spread(NS - 1, 1)
                    for n in range(NS - 4, NS):
                        reduce(n, n % 2, last=(n == NS - 1))

        @block.vector
        def _(dve):
            dve.sem_inc(u_ready, 2)
            dve.sem_inc(h_ready, A0)
            dve.sem_inc(v_free, 2)
            dve.memset(u[:, 0], 0.0).then_inc(zero_ready, 1)
            dve.memset(ones[:], 1.0).then_inc(ones_ready, 1)
            dve.wait_ge(consts, 48)
            for q in range(Q):
                dve.tensor_scalar(dd[:, q, :], ident[:], dcol[:, q:q + 1], None, ALU.mult).then_inc(dd_ready, 1)
            dve.wait_ge(y_zeroed, Q)
            with dve.Fori(0, B) as b:
                dve.wait_ge(carry_saved, b * (KC * NS) + 1)
                dve.memset(carry[:], 0.0).then_inc(carry_zeroed, 1)
                dve.wait_ge(carry_zeroed, b + 1)
                hold(dve, ticks["dve"])
                with dve.Fori(0, KC // 2) as k:
                    for par in range(2):
                        p = b * (KC // 2) + k
                        c = p * 2 + par

                        def inputs(n, i):
                            g = c * NS + n
                            dve.wait_ge(bb_ready, g + 3)
                            dve.wait_ge(h_ready, g * Q + Q)
                            dve.tensor_tensor(u[:, i], v[:, par], bb_ps[:].rearrange("p (o t) -> p o t", o=1).broadcast_to([P, Q, T]), ALU.mult).then_inc(u_ready, 1)

                        def scans(n, i):
                            g = c * NS + n
                            dve.wait_ge(u_ready, g + 3)
                            dve.wait_ge(hc_ready, g + 1)
                            for q in range(Q):
                                dve.wait_ge(a_ready, g * Q + q + 1)
                                dve.tensor_tensor_scan(h[:, i, q, :], a_ps[:, q % A_SLOTS, :], u[:, i, q, :],
                                                       carry[:, bass.ds(n, 1), q], ALU.mult, ALU.add).then_inc(h_ready, 1)

                        dve.wait_ge(v_in[par], (p + 1) * 16)
                        inputs(0, 0)
                        inputs(1, 1)
                        with dve.Fori(0, NS // 2 - 1) as m:
                            for i in range(2):
                                scans(m * 2 + i, i)
                                inputs(m * 2 + 2 + i, i)
                        dve.wait_ge(u_ready, c * NS + NS + 2)
                        dve.sem_inc(v_free, 1)
                        scans(NS - 2, 0)
                        scans(NS - 1, 1)


def mid_phase(nc, NCH, D, x_d, y_s, wout_d, w0_d, b0_d, ns_d, nb_d, wx_d, ww_d, bw_d, wk_d, wr_d, wv_d, ident_d, x2_s, a_s, k_s, r_s, v_s):
    Q = D // P
    J = T // P
    with ExitStack() as ctx:
        sb = lambda n, s: ctx.enter_context(nc.sbuf_tensor("mid_" + n, s, F32))
        ps = lambda n, s: ctx.enter_context(nc.psum_tensor("mid_" + n, s, F32))
        sem = lambda n: ctx.enter_context(nc.semaphore("mid_" + n))
        pa = ps("pa", [P, Q, T]); pb = ps("pb", [P, Q, T])
        yt = sb("yt", [P, 2, Q, T]); x = sb("x", [P, 2, J, D]); x2 = sb("x2", [P, 2, J, D]); h = sb("h", [P, J, D])
        ht = sb("ht", [P, Q, T]); xnt = sb("xnt", [P, 2, Q, T]); hx = sb("hx", [P, Q, T])
        at = sb("at", [P, Q, T]); kt = sb("kt", [P, Q, T]); rt = sb("rt", [P, Q, T]); vv = sb("vv", [P, J, D])
        w = {n: sb(n, [P, Q, D]) for n in ("wout", "w0", "wx", "ww", "wk", "wr", "wv")}
        b0 = sb("b0", [1, D]); ones = sb("ones", [1, P]); ident = sb("ident", [P, P])
        ns = sb("ns", [P, Q]); nb = sb("nb", [P, Q]); bw = sb("bw", [P, Q]); bwn = sb("bwn", [P, Q])
        st = sb("st", [P, J, 6]); mv = sb("mv", [P, J, 2]); ve = sb("ve", [P, J])
        half_neg = sb("half_neg", [P, J]); r0 = sb("r0", [P, J]); rr = sb("rr", [P, J]); tmp = sb("tmp", [P, J])
        consts = sem("consts"); ticks_dve = sem("ticks_dve"); half_ready = sem("half_ready"); small_ready = sem("small_ready"); bwn_ready = sem("bwn_ready")
        y_in = [sem(f"y_in{i}") for i in range(2)]
        x_in = [sem(f"x_in{i}") for i in range(2)]
        x2_out = [sem(f"x2_out{i}") for i in range(2)]
        outs = sem("outs")
        norm_steps = Count(sem("norm_steps"), 2 * J + 3 * NORM_DVE)
        root_steps = Count(sem("root_steps"), 3)
        turn_steps = Count(sem("turn_steps"), 2 * Q)
        ffn_steps = Count(sem("ffn_steps"), 2 * J + 2)
        proj_steps = Count(sem("proj_steps"), 5 * Q)
        actp_steps = Count(sem("actp_steps"), 3 * Q)
        dvep_steps = Count(sem("dvep_steps"), 2 * Q)
        S_X1, S_H, S_X2 = J, J + NORM_DVE, 2 * J + NORM_DVE
        xv = x_d.rearrange("(c j p) d -> c p j d", j=J, p=P)
        x2v = x2_s.rearrange("(c j p) d -> c p j d", j=J, p=P)
        vv_out = v_s.rearrange("(c j p) d -> c p j d", j=J, p=P)
        block = ctx.enter_context(nc.Block())

        @block.sync
        def _(sp):
            loads = [(w["wout"], wout_d), (w["w0"], w0_d), (w["wx"], wx_d), (w["ww"], ww_d), (w["wk"], wk_d), (w["wr"], wr_d), (w["wv"], wv_d),
                     (b0, b0_d), (ident, ident_d), (ns, ns_d), (nb, nb_d), (bw, bw_d)]
            for dst, src in loads:
                sp.dma_start(dst[:], src).then_inc(consts, 16)
            for par in range(2):
                sp.sem_inc(x2_out[par], 16)
            sp.sem_inc(outs, 64)

            def load(c, par, half):
                ffn_steps.wait_freed(sp, c)
                sp.dma_start(yt[:, par], y_s[c + 1]).then_inc(y_in[par], 16)
                sp.dma_start(x[:, par], xv[c]).then_inc(x_in[par], 16)

            def store_x2(c, par, half):
                norm_steps.wait(sp, c, S_X2)
                sp.dma_start(x2v[c], x2[:, par]).then_inc(x2_out[par], 16)

            def store(c, par, half):
                actp_steps.wait(sp, c, 2 * Q)
                sp.dma_start(a_s[c], at[:]).then_inc(outs, 16)
                dvep_steps.wait(sp, c, Q)
                sp.dma_start(k_s[c], kt[:]).then_inc(outs, 16)
                actp_steps.wait_all(sp, c)
                sp.dma_start(r_s[c], rt[:]).then_inc(outs, 16)
                dvep_steps.wait_all(sp, c)
                sp.dma_start(vv_out[c], vv[:]).then_inc(outs, 16)
            skewed(sp, NCH, [(1, load), (1, store_x2), (0, store)])
            for par in range(2):
                sp.wait_ge(x2_out[par], 16 * (NCH // 2 + 1))
            sp.wait_ge(outs, 64 * (NCH + 1))

        @block.gpsimd
        def _(pool):
            root_steps.start(pool)
            pool.memset(half_neg[:], -0.5).then_inc(half_ready, 1)
            pool.wait_ge(half_ready, 1)

            def roots(c, par, half):
                root_steps.begin(c)
                for n in (S_X1, S_X2, S_X2 + NORM_DVE):
                    root_pool(pool, root_steps, norm_steps, c, n + NORM_VE, r0[:], ve[:], half_neg[:])
            in_turn(pool, NCH, roots)

        @block.vector
        def _(dve):
            norm_steps.start(dve)
            dvep_steps.start(dve)
            dve.memset(ones[:], 1.0).then_inc(small_ready, 1)

            def norm(c, n, out, src):
                norm_dve(dve, ticks_dve, norm_steps, root_steps, c, n, out, src, st, mv, ve[:], r0[:], rr[:], tmp[:], J)

            def first_sum(c, par, half):
                norm_steps.begin(c)
                dve.wait_ge(x_in[par], (half + 1) * 16)
                for j in range(J):
                    ffn_steps.wait(dve, c, j + 1)
                    norm_steps.inc(dve.tensor_tensor(x[:, par, j, :], x[:, par, j, :], pa[:, j, :], ALU.add))
                norm_steps.wait(dve, c, S_X1)
                norm(c, 1, h, x[:, par])

            def second_sum(c, par, half):
                dve.wait_ge(x2_out[par], (half + 1) * 16)
                for j in range(J):
                    ffn_steps.wait(dve, c, J + 1 + j + 1)
                    norm_steps.inc(dve.tensor_tensor(x2[:, par, j, :], x[:, par, j, :], pa[:, j, :], ALU.add))

            def more_norms(c, par, half):
                norm_steps.wait(dve, c, S_X2)
                norm(c, 2, h, x2[:, par])
                norm(c, 3, x[:, par], h)

            def keys(c, par, half):
                dvep_steps.begin(c)
                dve.wait_ge(outs, (c + 1) * 64)
                for q in range(Q):
                    proj_steps.wait(dve, c, 2 * Q + q + 1)
                    dvep_steps.inc(dve.tensor_copy(kt[:, q, :], pb[:, q, :]))

            def values(c, par, half):
                for j in range(J):
                    proj_steps.wait(dve, c, 4 * Q + j + 1)
                    dvep_steps.inc(dve.tensor_copy(vv[:, j, :], pb[:, j, :]))
            skewed(dve, NCH, [(1, first_sum), (1, second_sum), (0, keys), (1, more_norms), (0, values)])

        @block.scalar
        def _(act):
            turn_steps.start(act)
            actp_steps.start(act)
            act.wait_ge(consts, 12 * 16)
            act.mul(bwn[:], bw[:], -1.0).then_inc(bwn_ready, 1)
            act.wait_ge(bwn_ready, 1)

            def low_rank(c, par, half):
                actp_steps.begin(c)
                for q in range(Q):
                    proj_steps.wait(act, c, q + 1)
                    actp_steps.inc(act.copy(hx[:, q, :], pb[:, q, :]))

            def turned_h(c, par, half):
                turn_steps.begin(c)
                ffn_steps.wait(act, c, J + 1)
                for q in range(Q):
                    turn_steps.inc(act.copy(ht[:, q, :], pa[:, q, :]))

            def gates(c, par, half):
                act.wait_ge(outs, (c + 1) * 64)
                for q in range(Q):
                    proj_steps.wait(act, c, Q + q + 1)
                    actp_steps.inc(act.activation(at[:, q, :], pb[:, q, :], ACT.Sigmoid, bias=bwn[:, q:q + 1], scale=-1.0))
                for q in range(Q):
                    proj_steps.wait(act, c, 3 * Q + q + 1)
                    actp_steps.inc(act.activation(rt[:, q, :], pb[:, q, :], ACT.Sigmoid))

            def turned_xn(c, par, half):
                proj_steps.wait_freed(act, c)
                ffn_steps.wait_all(act, c)
                for q in range(Q):
                    turn_steps.inc(act.activation(xnt[:, par, q, :], pa[:, q, :], ACT.Identity, bias=nb[:, q:q + 1], scale=ns[:, q:q + 1]))
            skewed(act, NCH, [(0, low_rank), (1, turned_h), (0, gates), (1, turned_xn)])

        @block.tensor
        def _(pe):
            ffn_steps.start(pe)
            proj_steps.start(pe)
            pe.wait_ge(consts, 12 * 16)
            pe.wait_ge(small_ready, 1)

            def attn_out(c, par, half):
                ffn_steps.begin(c)
                pe.wait_ge(y_in[par], (half + 1) * 16)
                turn_steps.wait_before(pe, c)
                for j in range(J):
                    for q in range(Q):
                        mm = pe.matmul(pa[:, j, :], yt[:, par, q, j * P:(j + 1) * P], w["wout"][:, q, :], start=(q == 0), stop=(q == Q - 1))
                    ffn_steps.inc(mm)

            def turn(src):
                for q in range(Q):
                    for j in range(J):
                        mm = pe.transpose(pa[:, q, j * P:(j + 1) * P], src[:, j, q * P:(q + 1) * P], ident[:])
                ffn_steps.inc(mm)

            def turn_h(c, par, half):
                norm_steps.wait(pe, c, S_H)
                turn(h)

            def ffn(c, par, half):
                turn_steps.wait(pe, c, Q)
                for j in range(J):
                    pe.matmul(pa[:, j, :], ones[:], b0[:], start=True, stop=False)
                    for q in range(Q):
                        mm = pe.matmul(pa[:, j, :], ht[:, q, j * P:(j + 1) * P], w["w0"][:, q, :], start=False, stop=(q == Q - 1))
                    ffn_steps.inc(mm)

            def turn_xn(c, par, half):
                norm_steps.wait_all(pe, c)
                turn(x[:, par])

            def columns(weight, src, free):
                for o in range(Q):
                    free(o)
                    for q in range(Q):
                        mm = pe.matmul(pb[:, o, :], w[weight][:, q, o * P:(o + 1) * P], src[:, q, :], start=(q == 0), stop=(q == Q - 1))
                    proj_steps.inc(mm)

            def low_rank(c, par, half):
                proj_steps.begin(c)
                turn_steps.wait_all(pe, c)
                dvep_steps.wait_before(pe, c)
                columns("wx", xnt[:, par], lambda o: None)

            def decay(c, par, half):
                actp_steps.wait(pe, c, Q)
                columns("ww", hx, lambda o: None)

            def keys_reads(c, par, half):
                columns("wk", xnt[:, par], lambda o: actp_steps.wait(pe, c, Q + o + 1))
                columns("wr", xnt[:, par], lambda o: dvep_steps.wait(pe, c, o + 1))

            def values(c, par, half):
                for j in range(J):
                    actp_steps.wait(pe, c, 2 * Q + j + 1)
                    for q in range(Q):
                        mm = pe.matmul(pb[:, j, :], xnt[:, par, q, j * P:(j + 1) * P], w["wv"][:, q, :], start=(q == 0), stop=(q == Q - 1))
                    proj_steps.inc(mm)
            skewed(pe, NCH, [(1, attn_out), (0, low_rank), (1, turn_h), (0, decay), (1, ffn), (0, keys_reads), (1, turn_xn), (0, values)])


SUB = 8
BIG = 3.0e38


def core_phase(nc, D, H, L, a_s, k_s, r_s, v_s, x2_s, wo_d, gam_d, bet_d, slopes_d, crow_d, trow_d, mask_d, hmask_d, ident_d, x3_s, oh_out, xs_out, ext_out):
    B = 2
    ITEMS = B * L // P
    Q = D // P
    NI = P // SUB
    W = SUB + 1
    LEVELS = (NI - 1).bit_length()
    pairs = [NI >> (l + 1) for l in range(LEVELS)]
    E_AT = [Q * sum(pairs[:l]) for l in range(LEVELS)]
    HP = P // 2
    E = D // H
    TPC = T // P
    with ExitStack() as ctx:
        sb = lambda n, s: ctx.enter_context(nc.sbuf_tensor("core_" + n, s, F32))
        ps = lambda n, s: ctx.enter_context(nc.psum_tensor("core_" + n, s, F32))
        sem = lambda n: ctx.enter_context(nc.semaphore("core_" + n))
        sc_ps = ps("sc_ps", [P, H, T // H]); at_ps = ps("at_ps", [P, 2, Q // 2, 2, P]); o_ps = ps("o_ps", [P, Q, P])
        kt_ps = ps("kt_ps", [P, Q, P]); su_ps = ps("su_ps", [P, Q, P]); y_ps = ps("y_ps", [P, D])
        a = sb("a", [P, 2, Q, P]); k = sb("k", [P, 2, Q, P]); r = sb("r", [P, 2, Q, P]); v = sb("v", [P, 2, D]); x = sb("x", [P, 2, D])
        rr = sb("rr", [P, SUB, Q * NI, W]); first = sb("first", [P, 2, Q * NI, W]); rk = sb("rk", [P, W, Q, P])
        ee = sb("ee", [P, 2, E_AT[-1] + Q, 4]); total = sb("total", [P, 2, Q, 1])
        kl = sb("kl", [P, 2, LEVELS, Q, P]); ql = sb("ql", [P, 2, LEVELS, Q, P])
        kz = sb("kz", [P, 2, 2, Q, P]); qb = sb("qb", [P, 2, LEVELS, Q, 2, HP])
        af = sb("af", [P, H, P]); ats = sb("ats", [P, 2, Q // 2, 2, P]); k8t = sb("k8t", [P, Q, P])
        ot = sb("ot", [P, Q, P]); s = sb("s", [P, 2, Q, P]); s1 = sb("s1", [P, Q, P])
        x3 = sb("x3", [P, 2, D]); z = sb("z", [P, 1, D]); zh = sb("zh", [P, 1, D]); xf = sb("xf", [P, D]); sg = sb("sg", [P, D]); pr = sb("pr", [P, D])
        wo = sb("wo", [P, Q, D]); gam = sb("gam", [P, D]); bet = sb("bet", [P, D]); sig = sb("sig", [P, D])
        NT = D // 8
        NCL = NT // 8
        crow = sb("crow", [P, NCL]); trow = sb("trow", [P, NT])
        mask = sb("mask", [P, P]); hmask = sb("hmask", [P, P]); ident = sb("ident", [P, P])
        st = sb("st", [P, 1, 6]); mv = sb("mv", [P, 1, 2]); ve = sb("ve", [P, 1]); half_neg = sb("half_neg", [P, 1]); r0 = sb("r0", [P, 1]); rt = sb("rt", [P, 1]); tmp = sb("tmp", [P, 1])
        ts = sb("ts", [P, NT]); cs = sb("cs", [P, NCL]); key = sb("key", [P, NT]); kmax = sb("kmax", [P, 1]); pen = sb("pen", [P, NT]); sel = sb("sel", [P, 2, NT])
        mm2 = sb("mm2", [P, 2])
        oh = sb("oh", [P, ITEMS, NT]); xs = sb("xs", [P, ITEMS, 8]); xsd = sb("xsd", [P, 8]); ext = sb("ext", [P, 2, NT])
        consts = sem("consts"); ticks_dve = sem("ticks_dve"); ticks_pool = sem("ticks_pool"); ticks_sp = sem("ticks_sp"); pool_ready = sem("pool_ready"); slope_sum = sem("slope_sum"); sig_ready = sem("sig_ready"); zeroed = sem("zeroed")
        ins_a = [sem(f"ins_a{i}") for i in range(2)]
        ins_b = [sem(f"ins_b{i}") for i in range(2)]
        x3_out = [sem(f"x3_out{i}") for i in range(2)]
        final = sem("final"); kmax_ready = sem("kmax_ready")
        chain = Count(sem("chain"), 1 + 2 * SUB)
        spread = Count(sem("spread"), 1)
        after = Count(sem("after"), 4 + 2 * NORM_DVE + 15)
        pool_a = Count(sem("pool_a"), (LEVELS + 1) + 2 * LEVELS)
        act_q = Count(sem("act_q"), 1 + LEVELS)
        sign = Count(sem("sign"), 1)
        A_TOTAL = LEVELS + 1
        pool_b = Count(sem("pool_b"), 2 + 4)
        act_a = Count(sem("act_a"), 3)
        pe_a = Count(sem("pe_a"), 1)
        pe_b = Count(sem("pe_b"), 5)
        S_X3 = 4
        S_N1, S_N2 = 4 + NORM_DVE, 4 + 2 * NORM_DVE

        GRID = slopes_d.shape[0] // D
        slopes = (qb[:].rearrange("p b l q h n -> p (b l q h n)")[:, 0:D * GRID // 2], ql[:].rearrange("p b l q n -> p (b l q n)")[:, 0:D * GRID // 2])

        def ones_and_decays(par, l):
            return ee[:, par, E_AT[l]:E_AT[l] + Q * pairs[l], :]

        block = ctx.enter_context(nc.Block())

        @block.sync
        def _(sp):
            for dst, src in ((wo, wo_d), (gam, gam_d.partition_broadcast(P)), (bet, bet_d.partition_broadcast(P)), (crow, crow_d), (trow, trow_d), (mask, mask_d),
                             (hmask, hmask_d), (ident, ident_d)):
                sp.dma_start(dst[:], src).then_inc(consts, 16)
            for half in range(2):
                sp.dma_start(slopes[half], slopes_d[half * D * GRID // 2:(half + 1) * D * GRID // 2].partition_broadcast(P)).then_inc(consts, 16)
            for par in range(2):
                sp.sem_inc(x3_out[par], 16)

            def load_decays(i, par, m):
                c = m // TPC + par * (L // T)
                t = m % TPC
                chain.wait_freed(sp, i)
                hold(sp, ticks_sp)
                pool_a.wait_freed(sp, i)
                hold(sp, ticks_sp)
                for dst, src in ((a, a_s), (k, k_s), (r, r_s)):
                    sp.dma_start(dst[:, par], src[c, :, :, bass.ds(t * P, P)]).then_inc(ins_a[par], 16)

            def load_rows(i, par, m):
                after.wait_freed(sp, i)
                hold(sp, ticks_sp)
                pe_b.wait_freed(sp, i)
                hold(sp, ticks_sp)
                sp.dma_start(v[:, par], v_s[bass.ds((m + par * (L // P)) * P, P), :]).then_inc(ins_b[par], 16)
                sp.dma_start(x[:, par], x2_s[bass.ds((m + par * (L // P)) * P, P), :]).then_inc(ins_b[par], 16)

            def store(i, par, m):
                after.wait(sp, i, S_N2 + 1)
                hold(sp, ticks_sp)
                sp.dma_start(x3_s[bass.ds((m + par * (L // P)) * P, P), :], x3[:, par]).then_inc(x3_out[par], 16)
            staggered(sp, ITEMS, [(1, load_rows), (2, load_decays), (0, store)])
            after.wait_all(sp, ITEMS - 1)
            sp.dma_start(oh_out, oh[:]).then_inc(final, 16)
            sp.dma_start(xs_out, xs[:]).then_inc(final, 16)
            sp.dma_start(ext_out, ext[:]).then_inc(final, 16)
            sp.wait_ge(final, 48)
            for par in range(2):
                sp.wait_ge(x3_out[par], 16 * (ITEMS // 2 + 1))

        @block.gpsimd
        def _(pool):
            pool_a.start(pool)
            pool_b.start(pool)
            pool.memset(half_neg[:], -0.5).then_inc(pool_ready, 1)
            pool.wait_ge(pool_ready, 1)
            pool.wait_ge(zeroed, 7)
            pool.wait_ge(consts, 160)
            pool.wait_ge(sig_ready, 1)

            def keys(i, par, m):
                pool_a.begin(i)
                pe_b.wait_freed(pool, i)
                hold(pool, ticks_pool)
                chain.wait_all(pool, i)
                hold(pool, ticks_pool)
                pool_a.link(pool, pool.tensor_scalar(ones_and_decays(par, 0)[:, :, 1:3], first[:, par, :, SUB].rearrange("p (c e) -> p c e", e=2), 1.0, None, ALU.mult))
                for l in range(LEVELS):
                    both = ones_and_decays(par, l)
                    if l + 1 < LEVELS:
                        both = both.rearrange("p (c e) w -> p c e w", e=2)
                        dst = ones_and_decays(par, l + 1)[:, :, 1:3]
                        pool_a.link(pool, pool.tensor_tensor(dst, both[:, :, :, 1], both[:, :, :, 2], ALU.mult))
                    else:
                        pool_a.link(pool, pool.tensor_tensor(total[:, par], both[:, :, 1:2], both[:, :, 2:3], ALU.mult))
                for l in range(LEVELS):
                    n = SUB << l
                    shape = [P, Q * pairs[l], 2, n]
                    e = ones_and_decays(par, l)
                    cut = lambda t: t.rearrange("p q (c e n) -> p (q c) e n", e=2, n=n)
                    key_in = cut(rk[:, SUB] if l == 0 else kl[:, par, l - 1])
                    read_in = first[:, par, :, 0:SUB].rearrange("p (c e) n -> p c e n", e=2) if l == 0 else cut(ql[:, par, l - 1])
                    pool_a.inc(pool.tensor_tensor(cut(kl[:, par, l]), key_in, e[:, :, 2:4].rearrange("p c (e n) -> p c e n", n=1).broadcast_to(shape), ALU.mult))
                    pool_a.link(pool, pool.tensor_tensor(cut(ql[:, par, l]), read_in, e[:, :, 0:2].rearrange("p c (e n) -> p c e n", n=1).broadcast_to(shape), ALU.mult))

            def route(i, par, m):
                pool_b.begin(i)
                for n in (S_X3, S_N1):
                    root_pool(pool, pool_b, after, i, n + NORM_VE, r0[:], ve[:], half_neg[:])
                after.wait(pool, i, S_N2)
                pool_b.link(pool, pool.tensor_tensor(xf[:], zh[:, 0], gam[:], ALU.mult))
                pool_b.inc(pool.tensor_tensor(xf[:], xf[:], bet[:], ALU.add))
                sign.wait_all(pool, i)
                pool_b.inc(pool.tensor_tensor(pr[:], sg[:], sig[:], ALU.mult))
                after.wait(pool, i, S_N2 + 7)
                pool_b.inc(pool.tensor_tensor(pr[:].rearrange("p (n e) -> p n e", e=8), xf[:].rearrange("p (n e) -> p n e", e=8),
                                              oh[:, bass.ds(par * (L // P) + m, 1), :].rearrange("p o (n e) -> p (o n) e", e=1).broadcast_to([P, NT, 8]), ALU.mult))
            staggered(pool, ITEMS, [(0, route), (2, keys)])

        @block.vector
        def _(dve):
            chain.start(dve)
            spread.start(dve)
            after.start(dve)
            dve.memset(kz[:], 0.0).then_inc(zeroed, 1)
            dve.wait_ge(consts, 160)
            for half in range(2):
                dve.tensor_reduce(sig[:, half * D // 2:(half + 1) * D // 2], slopes[half].rearrange("p (d g) -> p d g", g=GRID), AX.X, ALU.add).then_inc(slope_sum, 1)
            dve.wait_ge(slope_sum, 2)
            dve.memset(rk[:], 0.0).then_inc(zeroed, 1)
            dve.memset(s[:], 0.0).then_inc(zeroed, 1)
            dve.memset(ext[:], -BIG).then_inc(zeroed, 1)
            dve.memset(qb[:], 0.0).then_inc(zeroed, 1)
            dve.memset(ee[:], 1.0).then_inc(zeroed, 1)
            dve.memset(rr[:, SUB - 1, :, SUB:W], 1.0).then_inc(zeroed, 1)
            dve.wait_ge(zeroed, 7)
            dve.wait_ge(consts, 160)

            def decays(i, par, m):
                chain.begin(i)
                dve.wait_ge(ins_a[par], (m + 1) * 48)
                pool_a.wait_freed(dve, i)
                act_q.wait_freed(dve, i)
                chain.wait_before(dve, i)
                pe_a.wait_before(dve, i)
                pool_a.wait(dve, i - 1, A_TOTAL + 1)
                act_q.wait(dve, i - 1, 1)
                kv = k[:, par].rearrange("p q (i t) -> p t (q i)", t=SUB)
                av, rv = (w[:, par].rearrange("p q (i t) -> p (q i) t", t=SUB) for w in (a, r))
                for j in range(SUB):
                    last = dve.tensor_copy(rr[:, j, :, j:j + 1], rv[:, :, j:j + 1])
                chain.link(dve, last)
                for j in range(SUB - 1, -1, -1):
                    decayed = chain.inc(dve.tensor_tensor((rr[:, j - 1] if j else first[:, par])[:, :, j:W], rr[:, j, :, j:W], av[:, :, j:j + 1].broadcast_to([P, Q * NI, W - j]), ALU.mult))
                    chain.inc(dve.tensor_tensor(rk[:, j:W].rearrange("p t q (i j) -> p t (q i) j", j=SUB)[:, :, :, j],
                                                rr[:, j, :, j:W].rearrange("p c w -> p w c"), kv[:, j:j + 1].broadcast_to([P, W - j, Q * NI]), ALU.mult))
                    if j:
                        chain.wait(dve, i, decayed)

            def spread_scores(i, par, m):
                spread.begin(i)
                pe_a.wait_all(dve, i)
                pe_b.wait(dve, i - 1, 1)
                shape = [P, NI, SUB]
                for h in range(H):
                    last = dve.tensor_tensor(af[:, h].rearrange("p (i t) -> p i t", t=SUB), sc_ps[:, h:h + 1, 0:SUB].broadcast_to(shape),
                                             mask[:].rearrange("p (i t) -> p i t", t=SUB), ALU.mult)
                spread.inc(last)

            def state(i, par, m):
                after.begin(i)
                pe_b.wait(dve, i, 4)
                after.inc(dve.tensor_tensor(s1[:], su_ps[:], hmask[:].rearrange("p (o e) -> p o e", o=1).broadcast_to([P, Q, P]), ALU.mult))
                after.link(dve, dve.tensor_tensor(s[:, par], s[:, par], total[:, par].broadcast_to([P, Q, P]), ALU.mult))
                after.inc(dve.tensor_tensor(s[:, par], s[:, par], s1[:], ALU.add))
                pe_b.wait_all(dve, i)
                dve.wait_ge(ins_b[par], (m + 1) * 32)
                dve.wait_ge(x3_out[par], (m + 1) * 16)
                after.link(dve, dve.tensor_tensor(x3[:, par], x[:, par], y_ps[:], ALU.add))

            def norms(i, par, m):
                norm_dve(dve, ticks_dve, after, pool_b, i, 1, z, x3[:, par:par + 1], st, mv, ve[:], r0[:], rt[:], tmp[:], 1)
                norm_dve(dve, ticks_dve, after, pool_b, i, 2, zh, z, st, mv, ve[:], r0[:], rt[:], tmp[:], 1)
                after.inc(dve.tensor_tensor(x3[:, par], x3[:, par], z[:, 0], ALU.add))

            def route(i, par, m):
                pool_b.wait(dve, i, 5)
                after.link(dve, dve.tensor_reduce(ts[:], pr[:].rearrange("p (n e) -> p n e", e=8), AX.X, ALU.add))
                after.link(dve, dve.tensor_reduce(cs[:], ts[:].rearrange("p (n e) -> p n e", e=8), AX.X, ALU.add))
                after.inc(dve.scalar_tensor_tensor(out=key[:], in0=ts[:], scalar=64.0, in1=trow[:], op0=ALU.mult, op1=ALU.add))
                after.link(dve, dve.scalar_tensor_tensor(out=cs[:], in0=cs[:], scalar=32768.0, in1=crow[:], op0=ALU.mult, op1=ALU.add))
                kv = key[:].rearrange("p (n e) -> p n e", e=8)
                dve.tensor_tensor(kv, kv, cs[:].rearrange("p (n e) -> p n e", e=1).broadcast_to([P, NCL, 8]), ALU.add).then_inc(after.sem, 1)
                after.n += 1
                after.wait(dve, i, after.n)
                dve.tensor_reduce(kmax[:], key[:], AX.X, ALU.max).then_inc(kmax_ready, 1)
                dve.wait_ge(kmax_ready, i + 1)
                after.link(dve, dve.tensor_scalar(oh[:, bass.ds(par * (L // P) + m, 1), :].rearrange("p o n -> p (o n)"), key[:], kmax[:, 0:1], None, ALU.is_equal))
                ohi = oh[:, bass.ds(par * (L // P) + m, 1), :].rearrange("p o n -> p (o n)")
                after.inc(dve.tensor_scalar(pen[:], ohi, -BIG, BIG, ALU.mult, ALU.add))
                pool_b.wait_all(dve, i)
                xsi = xsd[:]
                after.link(dve, dve.tensor_reduce(xsi, pr[:].rearrange("p (n e) -> p e n", e=8), AX.X, ALU.add))
                after.inc(dve.tensor_scalar(xs[:, bass.ds(par * (L // P) + m, 1), :].rearrange("p o n -> p (o n)"), xsi, 1.0, None, ALU.mult))
                after.inc(dve.tensor_reduce(mm2[:, 0:1], xsi, AX.X, ALU.max))
                after.link(dve, dve.tensor_reduce(mm2[:, 1:2], xsi, AX.X, ALU.min, negate=True))
                for e in range(2):
                    last = dve.scalar_tensor_tensor(out=sel[:, e, :], in0=ohi, scalar=mm2[:, e:e + 1], in1=pen[:], op0=ALU.mult, op1=ALU.subtract)
                    after.inc(last)
                after.wait(dve, i, after.n)
                after.link(dve, dve.tensor_tensor(ext[:], ext[:], sel[:], ALU.max))
            staggered(dve, ITEMS, [(0, state), (1, spread_scores), (0, norms), (2, decays), (0, route)])

        @block.scalar
        def _(act):
            act_a.start(act)
            act.wait_ge(slope_sum, 2)
            act.activation(sig[:], sig[:], ACT.Sign, scale=1.0 / GRID).then_inc(sig_ready, 1)

            act_q.start(act)
            sign.start(act)
            act.wait_ge(zeroed, 7)

            def by_head(i, par, m):
                act_q.begin(i)
                pe_b.wait_freed(act, i)
                chain.wait_all(act, i)
                for odd in range(2):
                    cut = lambda t: t.rearrange("p q (c e n) -> p (q c) e n", e=4, n=SUB)[:, :, 2 * odd, :]
                    last = act.copy(cut(kz[:, par, odd]), cut(rk[:, SUB]))
                act_q.inc(last)
                for l in range(LEVELS):
                    n = SUB << l
                    if l == 0:
                        src = first[:, par, :, 0:SUB].rearrange("p (q c e) n -> p q c e n", e=2, q=Q)[:, :, :, 1]
                    else:
                        pool_a.wait(act, i, A_TOTAL + 2 * l)
                        src = ql[:, par, l - 1].rearrange("p q (c e n) -> p q c e n", e=2, n=n)[:, :, :, 1]
                    for h2 in range(2):
                        lo = h2 * E
                        last = act.copy(qb[lo:lo + E, par, l, :, h2, :].rearrange("p q (c n) -> p q c n", n=n), src[lo:lo + E])
                    act_q.inc(last)

            def evac(i, par, m):
                act_a.begin(i)
                pe_b.wait(act, i, 1)
                for g in range(2):
                    last = act.copy(ats[:, g], at_ps[:, g])
                act_a.inc(last)
                pe_b.wait(act, i, 2)
                act_a.inc(act.copy(k8t[:], kt_ps[:]))
                pe_b.wait(act, i, 3)
                act_a.inc(act.copy(ot[:], o_ps[:]))

            def signs(i, par, m):
                sign.begin(i)
                pool_b.wait(act, i, 4)
                sign.inc(act.activation(sg[:], xf[:], ACT.Sign))
            staggered(act, ITEMS, [(1, by_head), (1, evac), (0, signs)])

        @block.tensor
        def _(pe):
            pe_a.start(pe)
            pe_b.start(pe)
            pe.wait_ge(consts, 160)
            pe.wait_ge(zeroed, 7)

            def scores(i, par, m):
                pe_a.begin(i)
                spread.wait_before(pe, i)
                chain.wait_all(pe, i)
                for t in range(SUB):
                    for q in range(Q):
                        mm = pe.matmul(sc_ps[:, 2 * q:2 * q + 2, t], rk[:, t, q, :], hmask[:, 0:P:E], start=True, stop=True)
                pe_a.inc(mm)

            def attend(i, par, m):
                pe_b.begin(i)
                spread.wait_all(pe, i)
                pool_a.wait_all(pe, i)
                act_q.wait_all(pe, i)
                act_a.wait_before(pe, i)
                for g in range(2):
                    pe.matmul(at_ps[:, g], ident[:], af[:, g * (H // 2):(g + 1) * (H // 2), :], start=True, stop=True)
                for q in range(Q):
                    to = at_ps[:, q // 2, q % 2]
                    for l in range(LEVELS):
                        n = SUB << l
                        for c in range(pairs[l]):
                            at, reads = 2 * n * c, qb[:, par, l, q, :, n * c:n * (c + 1)]
                            lo, rows = (at, n) if l else (at // 32 * 32, 32)
                            keys = kz[:, par, c % 2, q, lo:lo + rows] if l == 0 else kl[:, par, l - 1, q, lo:lo + rows]
                            mm = pe.matmul(to[lo:lo + rows, :, at + n:at + 2 * n], keys, reads, start=False, stop=True, skip_group_check=True, tile_position=(0, lo))
                pe_b.inc(mm)
                for q in range(Q):
                    mm = pe.transpose(kt_ps[:, q, :], kl[:, par, LEVELS - 1, q, :], ident[:])
                pe_b.inc(mm)
                pe.wait_ge(ins_b[par], (m + 1) * 32)
                after.wait_freed(pe, i)
                act_a.wait(pe, i, 1)
                for q in range(Q):
                    pe.matmul(o_ps[:, q, :], s[:, par, q, :], ql[:, par, LEVELS - 1, q, :], start=True, stop=True)
                    for h2 in range(2):
                        h = 2 * q + h2
                        mm = pe.matmul(o_ps[h2 * E:(h2 + 1) * E, q, :], v[:, par, h * E:(h + 1) * E], ats[:, q // 2, q % 2, h2, :], start=False, stop=True, skip_group_check=True)
                pe_b.inc(mm)
                act_a.wait(pe, i, 2)
                after.wait(pe, i - 1, S_X3)
                for q in range(Q):
                    mm = pe.matmul(su_ps[:, q, :], k8t[:, q, :], v[:, par, q * P:(q + 1) * P], start=True, stop=True)
                pe_b.inc(mm)
                act_a.wait(pe, i, 3)
                for q in range(Q):
                    mm = pe.matmul(y_ps[:], ot[:, q, :], wo[:, q, :], start=(q == 0), stop=(q == Q - 1))
                pe_b.inc(mm)
            staggered(pe, ITEMS, [(0, attend), (1, scores)])


def final_phase(nc, D, N, x3_s, oh_s, xs_s, ext_s, table_d, grid_d, ident_d, out_d):
    NT, GRID = oh_s.shape[2], 16
    TILES = N // P
    NCH = N // T
    J = T // P
    SL = D // NT
    TW = 2 * SL * GRID + 1
    TOP = 1.0 - 1e-6
    with ExitStack() as ctx:
        sb = lambda n, s: ctx.enter_context(nc.sbuf_tensor("fin_" + n, s, F32))
        ps = lambda n, s: ctx.enter_context(nc.psum_tensor("fin_" + n, s, F32))
        sem = lambda n: ctx.enter_context(nc.semaphore("fin_" + n))
        rows = ps("rows", [P, 2, J, T])
        oh = sb("oh", [P, TILES, NT]); xs = sb("xs", [P, TILES, SL]); ext = sb("ext", [P, 2, NT]); exta = sb("exta", [P, 2, NT])
        pr = sb("pr", [P, TILES, NT]); lim = sb("lim", [P, 2, TILES]); diff = sb("diff", [P, TILES]); rec = sb("rec", [P, TILES])
        u = sb("u", [P, TILES, SL]); u16 = sb("u16", [P, TILES, SL]); gi = sb("gi", [P, TILES, SL])
        ge = sb("ge", [P, TILES, SL, GRID + 1]); hot = sb("hot", [P, TILES, SL, GRID])
        grid = sb("grid", [P, GRID + 1]); table = sb("table", [NT, TW]); ident = sb("ident", [P, P])
        ohc = sb("ohc", [P, 2, J, NT]); oht = sb("oht", [NT, 2, J, P]); wv = sb("wv", [P, J, 2, SL * GRID]); bs = sb("bs", [P, J, 2, SL])
        delta = sb("delta", [P, 2, J, SL]); x = sb("x", [P, 2, J, D]); add = sb("add", [P, 2, J, D])
        consts = sem("consts"); ticks_act = sem("ticks_act"); pre = sem("pre"); ext_all = sem("ext_all")
        x_in = [sem(f"x_in{i}") for i in range(2)]
        out = [sem(f"out{i}") for i in range(2)]
        turned = Count(sem("turned"), 2)
        copied = Count(sem("copied"), 1); staged = Count(sem("staged"), 1)
        spline = Count(sem("spline"), 5)
        summed = Count(sem("summed"), 1)
        placed = Count(sem("placed"), 1)
        xv = x3_s.rearrange("(c j p) d -> c p j d", j=J, p=P)
        ov = out_d.rearrange("(c j p) d -> c p j d", j=J, p=P)
        block = ctx.enter_context(nc.Block())

        @block.sync
        def _(sp):
            for dst, src in ((ext, ext_s), (oh, oh_s), (xs, xs_s), (grid, grid_d), (table, table_d), (ident, ident_d)):
                sp.dma_start(dst[:], src).then_inc(consts, 16)
            for par in range(2):
                sp.sem_inc(out[par], 16)

            def load(c, par, half):
                sp.wait_ge(out[par], (half + 1) * 16)
                sp.dma_start(x[:, par], xv[c]).then_inc(x_in[par], 16)

            def store(c, par, half):
                summed.wait_all(sp, c)
                sp.dma_start(ov[c], x[:, par]).then_inc(out[par], 16)
            skewed(sp, NCH, [(1, load), (0, store)])
            for par in range(2):
                sp.wait_ge(out[par], 16 * (NCH // 2 + 1))

        @block.gpsimd
        def _(pool):
            placed.start(pool)
            pool.wait_ge(consts, 96)
            pool.partition_all_reduce(exta[:].rearrange("p e n -> p (e n)"), ext[:].rearrange("p e n -> p (e n)"), P, bass.bass_isa.ReduceOp.max).then_inc(ext_all, 1)

            def place(c, par, half):
                placed.begin(c)
                spline.wait_all(pool, c)
                summed.wait_freed(pool, c)
                for j in range(J):
                    last = pool.tensor_tensor(add[:, par, j].rearrange("p (n e) -> p n e", e=SL), oh[:, bass.ds(c * J + j, 1), :].rearrange("p o (n e) -> p (o n) e", e=1).broadcast_to([P, NT, SL]),
                                              delta[:, par, j:j + 1, :].broadcast_to([P, NT, SL]), ALU.mult)
                placed.inc(last)
            in_turn(pool, NCH, place)

        @block.vector
        def _(dve):
            spline.start(dve)
            summed.start(dve)
            count = [0]

            def link(ins):
                count[0] += 1
                ins.then_inc(pre, 1)
                dve.wait_ge(pre, count[0])
            dve.wait_ge(consts, 96)
            dve.wait_ge(ext_all, 1)
            for e in range(2):
                link(dve.tensor_tensor(pr[:], oh[:], exta[:, e:e + 1, :].broadcast_to([P, TILES, NT]), ALU.mult))
                link(dve.tensor_reduce(lim[:, e, :], pr[:], AX.X, ALU.add))
            link(dve.scalar_tensor_tensor(out=diff[:], in0=lim[:, 0, :], scalar=1.0, in1=lim[:, 1, :], op0=ALU.mult, op1=ALU.add))
            link(dve.tensor_scalar(diff[:], diff[:], 1e-8, None, ALU.add))
            link(dve.reciprocal(rec[:], diff[:]))
            wide = [P, TILES, SL]
            link(dve.tensor_tensor(u[:], xs[:], lim[:, 1, :].rearrange("p (t o) -> p t o", o=1).broadcast_to(wide), ALU.add))
            link(dve.tensor_tensor(u[:], u[:], rec[:].rearrange("p (t o) -> p t o", o=1).broadcast_to(wide), ALU.mult))
            link(dve.tensor_scalar(u[:], u[:], 0.0, TOP, ALU.max, ALU.min))
            link(dve.tensor_scalar(u16[:], u[:], float(GRID), None, ALU.mult))
            flat = lambda t: t[:].rearrange("p t e -> p (t e)")
            link(dve.tensor_tensor(ge[:].rearrange("p t e g -> p (t e) g"), flat(u16).rearrange("p (t o) -> p t o", o=1).broadcast_to([P, TILES * SL, GRID + 1]),
                                   grid[:].rearrange("p (o g) -> p o g", o=1).broadcast_to([P, TILES * SL, GRID + 1]), ALU.is_ge))
            g3 = ge[:].rearrange("p t e g -> p (t e) g")
            link(dve.tensor_tensor(hot[:].rearrange("p t e g -> p (t e) g"), g3[:, :, 0:GRID], g3[:, :, 1:GRID + 1], ALU.subtract))
            link(dve.tensor_reduce(flat(gi), g3[:, :, 1:GRID], AX.X, ALU.add))
            link(dve.scalar_tensor_tensor(out=u16[:], in0=gi[:], scalar=-1.0 / GRID, in1=u[:], op0=ALU.mult, op1=ALU.add))
            link(dve.tensor_scalar(u16[:], u16[:], float(GRID), None, ALU.mult))

            def splines(c, par, half):
                spline.begin(c)
                turned.wait_all(dve, c)
                placed.wait_freed(dve, c)
                for j in range(J):
                    last = dve.tensor_tensor(wv[:, j], rows[:, par, j, 0:TW - 1].rearrange("p (k g) -> p k g", k=2),
                                             hot[:, bass.ds(c * J + j, 1)].rearrange("p o e g -> p o (e g)").broadcast_to([P, 2, SL * GRID]), ALU.mult)
                spline.link(dve, last)
                spline.link(dve, dve.tensor_reduce(bs[:].rearrange("p j k e -> p (j k e)"), wv[:].rearrange("p j k (e g) -> p (j k e) g", g=GRID), AX.X, ALU.add))
                d = delta[:, par]
                spline.link(dve, dve.tensor_tensor(d, bs[:, :, 1, :], u16[:, bass.ds(c * J, J), :], ALU.mult))
                spline.link(dve, dve.tensor_tensor(d, d, bs[:, :, 0, :], ALU.add))
                spline.inc(dve.tensor_tensor(d, d, rows[:, par, :, TW - 1:TW].broadcast_to([P, J, SL]), ALU.mult))

            def sums(c, par, half):
                summed.begin(c)
                placed.wait_all(dve, c)
                dve.wait_ge(x_in[par], (half + 1) * 16)
                summed.inc(dve.tensor_tensor(x[:, par], x[:, par], add[:, par], ALU.add))
            skewed(dve, NCH, [(1, splines), (0, sums)])

        @block.scalar
        def _(act):
            copied.start(act)
            staged.start(act)
            act.wait_ge(consts, 96)

            def copy(c, par, half):
                copied.begin(c)
                turned.wait(act, c, 1)
                copied.inc(act.copy(oht[:, par], rows[0:NT, par, :, T - P:T]))

            def stage(c, par, half):
                staged.begin(c)
                turned.wait_freed(act, c)
                hold(act, ticks_act)
                staged.inc(act.copy(ohc[:, par], oh[:, bass.ds(c * J, J), :]))
            skewed(act, NCH, [(1, stage), (0, copy)])

        @block.tensor
        def _(pe):
            turned.start(pe)
            pe.wait_ge(consts, 96)

            def look_up(c, par, half):
                turned.begin(c)
                spline.wait_freed(pe, c)
                staged.wait_all(pe, c)
                for j in range(J):
                    mm = pe.matmul(rows[0:NT, par, j, T - P:T], ohc[:, par, j, :], ident[:], start=True, stop=True)
                turned.inc(mm)
                copied.wait_all(pe, c)
                for j in range(J):
                    mm = pe.matmul(rows[:, par, j, 0:TW], oht[:, par, j, :], table[:], start=True, stop=True)
                turned.inc(mm)

            in_turn(pe, NCH, look_up)


def program(nc, x, a_log, d_col, norm_w, norm_b, x_proj, dt_proj, dt_bias, out_proj, ffn_w, ffn_b,
            ln_scale, ln_bias, wx, ww, bw, wk, wv, wr, wo, gamma, beta, slopes, table,
            ident, cluster_row, tile_row, sub_mask, head_mask, grid, out):
    B, L, D = x.shape
    N = B * L
    NCH = N // T
    Q = D // P
    scratch = lambda name, shape: nc.dram_tensor("scratch_" + name, shape, F32, kind="Internal").ap()
    by_column = [NCH, P, Q, T]
    x_rows = x.rearrange("b l d -> (b l) d")
    dt_s, v_s, z_s = (scratch(n, by_column) for n in ("dt", "v", "z"))
    y_s = scratch("y", [NCH + 1, P, Q, T])
    bc_s = scratch("bc", [NCH, P, T])
    x2_s, vv_s, x3_s = (scratch(n, [N, D]) for n in ("x2", "vv", "x3"))
    NT = table.shape[0]
    oh_s = scratch("oh", [P, N // P, NT])
    xs_s = scratch("xs", [P, N // P, D // NT])
    ext_s = scratch("ext", [P, 2, NT])
    a_s, k_s, r_s = (scratch(n, by_column) for n in ("a", "k", "r"))

    pre_phase(nc, NCH, D, x_rows, x_proj, dt_proj, norm_w, norm_b, dt_bias, ident, dt_s, v_s, z_s, bc_s)
    scan_phase(nc, B, L, a_log, d_col, ident, dt_s, v_s, z_s, bc_s, y_s)
    mid_phase(nc, NCH, D, x_rows, y_s, out_proj, ffn_w, ffn_b, ln_scale, ln_bias, wx, ww, bw, wk, wr, wv, ident, x2_s, a_s, k_s, r_s, vv_s)
    core_phase(nc, D, HEADS, L, a_s, k_s, r_s, vv_s, x2_s, wo, gamma, beta, slopes, cluster_row, tile_row, sub_mask, head_mask, ident, x3_s, oh_s, xs_s, ext_s)
    final_phase(nc, D, N, x3_s, oh_s, xs_s, ext_s, table, grid, ident, out.rearrange("b l d -> (b l) d"))


def kernel(**inputs):
    import numpy as _np
    import concourse.bacc as _bacc
    from concourse import mybir as _mybir
    from concourse.bass_utils import run_bass_kernel_spmd as _run

    f = {n: _np.asarray(a) for n, a in inputs.items()}
    rows = lambda a: _np.ascontiguousarray(a.reshape(a.shape[0] // P, P, -1).transpose(1, 0, 2))
    turned = lambda a: rows(a.T)
    column = lambda a: _np.ascontiguousarray(a.reshape(-1, P).T)
    D = f["L0_attn_x"].shape[2]
    NT = f["L1_ffn_output_scale"].shape[0]
    SL = D // NT
    p = _np.arange(P)
    const = lambda row: _np.ascontiguousarray(_np.broadcast_to(row.astype(_np.float32), (P, row.shape[-1])))
    arrays = {
        "x": f["L0_attn_x"],
        "a_log": rows(f["L0_attn_A_log"]),
        "d_col": column(f["L0_attn_D_param"]),
        "norm_w": column(f["L0_attn_norm_w"]),
        "norm_b": column(f["L0_attn_norm_b"]),
        "x_proj": turned(f["L0_attn_x_proj_w"]),
        "dt_proj": _np.ascontiguousarray(f["L0_attn_dt_proj_w"].T),
        "dt_bias": column(f["L0_attn_dt_proj_b"]),
        "out_proj": turned(f["L0_attn_out_proj_w"]),
        "ffn_w": turned(f["L0_ffn_expert_w"][0]),
        "ffn_b": f["L0_ffn_expert_b"][0:1],
        "ln_scale": column(f["L1_attn_ln_scale"]),
        "ln_bias": column(f["L1_attn_ln_bias"]),
        "wx": turned(f["L1_attn_Wx"]),
        "ww": turned(f["L1_attn_Ww"]),
        "bw": column(f["L1_attn_bw"]),
        "wk": turned(f["L1_attn_Wk"]),
        "wv": turned(f["L1_attn_Wv"]),
        "wr": turned(f["L1_attn_Wr"]),
        "wo": turned(f["L1_attn_Wo"]),
        "gamma": f["L1_ffn_ln_gamma"],
        "beta": f["L1_ffn_ln_beta"],
        "slopes": f["L1_ffn_spline_slopes"].reshape(-1),
        "table": _np.concatenate([f["L1_ffn_spline_bases"].reshape(NT, -1), f["L1_ffn_spline_slopes"].reshape(NT, -1),
                                  f["L1_ffn_output_scale"].reshape(NT, 1)], axis=1),
        "ident": _np.eye(P, dtype=_np.float32),
        "cluster_row": const(-2048.0 * _np.arange(NT // SL)),
        "tile_row": const(-1.0 * _np.arange(NT)),
        "sub_mask": (p[:, None] // SUB == p[None] // SUB).astype(_np.float32),
        "head_mask": (p[:, None] // (D // HEADS) == p[None] // (D // HEADS)).astype(_np.float32),
        "grid": const(_np.arange(f["L1_ffn_spline_bases"].shape[2] + 1)),
    }
    nc = _bacc.Bacc("TRN2", target_bir_lowering=False, num_devices=1)
    held, args = {}, {}
    for name, a in arrays.items():
        a = _np.ascontiguousarray(a)
        held["in_" + name] = a
        args[name] = nc.dram_tensor("in_" + name, a.shape, _mybir.dt.from_np(a.dtype), kind="ExternalInput").ap()
    args["out"] = nc.dram_tensor("out_0", f["L0_attn_x"].shape, F32, kind="ExternalOutput").ap()
    program(nc, **args)
    r = _run(nc, [held], core_ids=[0])
    return r.results[0]["out_0"]
```

```python
from contextlib import ExitStack
import concourse.bass as bass
from concourse import mybir
ALU = mybir.AluOpType
ACT = mybir.ActivationFunctionType
AX = mybir.AxisListType
F32 = mybir.dt.float32
P = 128
T = 512
EPS = 1e-5
HEADS = 8


class Count:

    def __init__(self, sem, per):
        self.sem, self.per, self.n, self.item = sem, per, 0, 0

    def start(self, eng):
        eng.sem_inc(self.sem, 2 * self.per)

    def begin(self, item):
        assert self.n in (0, self.per), (self.sem, self.n)
        self.item, self.n = item, 0

    def inc(self, ins):
        self.n += 1
        assert self.n <= self.per, self.sem
        ins.then_inc(self.sem, 1)
        return self.n

    def link(self, eng, ins):
        self.inc(ins)
        eng.wait_ge(self.sem, (self.item + 2) * self.per + self.n)

    def wait(self, eng, item, n):
        eng.wait_ge(self.sem, (item + 2) * self.per + n)

    def wait_freed(self, eng, item):
        eng.wait_ge(self.sem, (item + 1) * self.per)

    def wait_before(self, eng, item):
        eng.wait_ge(self.sem, (item + 2) * self.per)

    def wait_all(self, eng, item):
        eng.wait_ge(self.sem, (item + 3) * self.per)


def skewed(eng, items, pieces):

    def turn(m, par, ahead=True, behind=True):
        for lead, piece in pieces:
            if lead and ahead:
                piece(m * 2 + par + 1, 1 - par, m + par)
            if not lead and behind:
                piece(m * 2 + par, par, m)

    for lead, piece in pieces:
        if lead:
            piece(0, 0, 0)
    if items > 2:
        with eng.Fori(0, items // 2 - 1) as m:
            turn(m, 0)
            turn(m, 1)
    turn(items // 2 - 1, 0)
    turn(items // 2 - 1, 1, ahead=False)


def staggered(eng, items, pieces):

    def turn(m, par, most=2):
        for lead, piece in pieces:
            if lead <= most:
                piece(m * 2 + par + lead, (par + lead) % 2, m + (par + lead) // 2)

    for before in (2, 1):
        for lead, piece in pieces:
            if lead >= before:
                piece(lead - before, (lead - before) % 2, 0)
    if items > 2:
        with eng.Fori(0, items // 2 - 1) as m:
            turn(m, 0)
            turn(m, 1)
    turn(items // 2 - 1, 0, 1)
    turn(items // 2 - 1, 1, 0)


def in_turn(eng, items, only):
    with eng.Fori(0, items // 2) as m:
        for par in range(2):
            only(m * 2 + par, par, m)


NORM_DVE = 8
NORM_VE = 3


def hold(eng, ticks):
    eng.sem_inc(ticks, 1)


def norm_dve(dve, ticks, cnt, roots, item, root_n, out, x, st, mv, ve, r0, rr, tmp, tiles):
    for j in range(tiles):
        last = dve.bn_stats(st[:, j, :], x[:, j, :])
    cnt.link(dve, last)
    hold(dve, ticks)
    for j in range(tiles):
        last = dve.bn_aggr(mv[:, j, :], st[:, j, :])
    cnt.link(dve, last)
    cnt.inc(dve.tensor_scalar(ve, mv[:, :, 1], EPS, None, ALU.add))
    roots.wait(dve, item, root_n)
    cnt.link(dve, dve.tensor_tensor(tmp, r0, r0, ALU.mult))
    cnt.link(dve, dve.tensor_tensor(tmp, tmp, ve, ALU.mult))
    cnt.link(dve, dve.tensor_scalar(tmp, tmp, -0.5, 1.5, ALU.mult, ALU.add))
    cnt.link(dve, dve.tensor_tensor(rr, r0, tmp, ALU.mult))
    for j in range(tiles):
        last = dve.tensor_scalar(out[:, j, :], x[:, j, :], mv[:, j, 0:1], rr[:, j:j + 1], ALU.subtract, ALU.mult)
    cnt.link(dve, last)


def root_pool(pool, cnt, stats, item, stats_n, r0, ve, neg_half):
    stats.wait(pool, item, stats_n)
    cnt.inc(pool.tensor_tensor(r0, ve, neg_half, ALU.pow))


def pre_phase(nc, NCH, D, x_d, xp_d, dtw_d, nw_d, nb_d, dtb_d, ident_d, dt_s, v_s, z_s, bc_s):
    Q = D // P
    J = T // P
    with ExitStack() as ctx:
        sb = lambda n, s: ctx.enter_context(nc.sbuf_tensor("pre_" + n, s, F32))
        ps = lambda n, s: ctx.enter_context(nc.psum_tensor("pre_" + n, s, F32))
        sem = lambda n: ctx.enter_context(nc.semaphore("pre_" + n))
        tp = ps("tp", [P, 2, Q, T])
        x = sb("x", [P, 2, J, D]); z = sb("z", [P, 2, J, D]); zh = sb("zh", [P, 2, J, D])
        zt = sb("zt", [P, 2, Q, T]); znt = sb("znt", [P, 2, Q, T])
        dl = sb("dl", [P, T]); bc = sb("bc", [P, 2, T])
        xb = sb("xb", [P, 2, Q, T]); ab = sb("ab", [P, 2, Q, T]); dt = sb("dt", [P, 2, Q, T]); v = sb("v", [P, 2, Q, T])
        st = sb("st", [P, J, 6]); mv = sb("mv", [P, J, 2]); ve = sb("ve", [P, J])
        half_neg = sb("half_neg", [P, J]); r0 = sb("r0", [P, J]); rr = sb("rr", [P, J]); tmp = sb("tmp", [P, J])
        xp = sb("xp", [P, Q, 2 * P]); dtw = sb("dtw", [P, D]); ident = sb("ident", [P, P])
        nw = sb("nw", [P, Q]); nb = sb("nb", [P, Q]); dtb = sb("dtb", [P, Q])
        consts = sem("consts"); ticks_dve = sem("ticks_dve"); half_ready = sem("half_ready")
        x_in = [sem(f"x_in{i}") for i in range(2)]
        outs = [sem(f"outs{i}") for i in range(2)]
        norm_steps = Count(sem("norm_steps"), 2 * NORM_DVE)
        root_steps = Count(sem("root_steps"), 2)
        proj_steps = Count(sem("proj_steps"), Q + 4)
        pe_steps = Count(sem("pe_steps"), 4 + Q)
        act_steps = Count(sem("act_steps"), 2 * Q + 3)
        xv = x_d.rearrange("(c j p) d -> c p j d", j=J, p=P)
        block = ctx.enter_context(nc.Block())

        @block.sync
        def _(sp):
            for dst, src in ((xp, xp_d), (dtw, dtw_d), (ident, ident_d), (nw, nw_d), (nb, nb_d), (dtb, dtb_d)):
                sp.dma_start(dst[:], src).then_inc(consts, 16)

            for par in range(2):
                sp.sem_inc(outs[par], 64)

            def load(c, par, half):
                norm_steps.wait_freed(sp, c)
                sp.dma_start(x[:, par], xv[c]).then_inc(x_in[par], 16)

            def store(c, par, half):
                proj_steps.wait(sp, c, Q + 2)
                sp.dma_start(z_s[c], zt[:, par]).then_inc(outs[par], 16)
                sp.dma_start(bc_s[c], bc[:, par]).then_inc(outs[par], 16)
                proj_steps.wait(sp, c, Q + 3)
                sp.dma_start(dt_s[c], dt[:, par]).then_inc(outs[par], 16)
                proj_steps.wait_all(sp, c)
                sp.dma_start(v_s[c], v[:, par]).then_inc(outs[par], 16)
            staggered(sp, NCH, [(2, load), (0, store)])
            for par in range(2):
                sp.wait_ge(outs[par], 64 * (NCH // 2 + 1))

        @block.gpsimd
        def _(pool):
            root_steps.start(pool)
            pool.memset(half_neg[:], -0.5).then_inc(half_ready, 1)
            pool.wait_ge(half_ready, 1)

            def roots(c, par, half):
                root_steps.begin(c)
                root_pool(pool, root_steps, norm_steps, c, NORM_VE, r0[:], ve[:], half_neg[:])
                root_pool(pool, root_steps, norm_steps, c, NORM_DVE + NORM_VE, r0[:], ve[:], half_neg[:])
            in_turn(pool, NCH, roots)

        @block.vector
        def _(dve):
            norm_steps.start(dve)
            proj_steps.start(dve)

            def first_norm(c, par, half):
                norm_steps.begin(c)
                dve.wait_ge(x_in[par], (half + 1) * 16)
                pe_steps.wait_freed(dve, c)
                norm_dve(dve, ticks_dve, norm_steps, root_steps, c, 1, z[:, par], x[:, par], st, mv, ve[:], r0[:], rr[:], tmp[:], J)

            def second_norm(c, par, half):
                norm_dve(dve, ticks_dve, norm_steps, root_steps, c, 2, zh[:, par], z[:, par], st, mv, ve[:], r0[:], rr[:], tmp[:], J)

            def turned(c, par, half):
                proj_steps.begin(c)
                dve.wait_ge(outs[par], (half + 1) * 64)
                pe_steps.wait(dve, c, 2)
                for q in range(Q):
                    proj_steps.inc(dve.tensor_copy(zt[:, par, q, :], tp[:, par, q, :]))

            def copies(c, par, half):
                pe_steps.wait(dve, c, 3)
                proj_steps.inc(dve.tensor_copy(dl[:], tp[:, par, 0, :]))
                pe_steps.wait(dve, c, 4)
                proj_steps.inc(dve.tensor_copy(bc[:, par, :], tp[:, par, 1, :]))

            def softplus(c, par, half):
                act_steps.wait_all(dve, c)
                proj_steps.link(dve, dve.scalar_tensor_tensor(out=dt[:, par], in0=xb[:, par], scalar=0.0, in1=ab[:, par], op0=ALU.max, op1=ALU.add))
                proj_steps.inc(dve.tensor_tensor(v[:, par], dt[:, par], znt[:, par], ALU.mult))
            skewed(dve, NCH, [(0, turned), (1, first_norm), (0, copies), (1, second_norm), (0, softplus)])

        @block.scalar
        def _(act):
            act_steps.start(act)
            act.wait_ge(consts, 96)

            def evac(c, par, half):
                act_steps.begin(c)
                proj_steps.wait_freed(act, c)
                pe_steps.wait(act, c, 1)
                for q in range(Q):
                    act_steps.inc(act.activation(znt[:, par, q, :], tp[:, par, q, :], ACT.Identity, bias=nb[:, q:q + 1], scale=nw[:, q:q + 1]))
                for q in range(Q):
                    pe_steps.wait(act, c, 5 + q)
                    act_steps.inc(act.activation(xb[:, par, q, :], tp[:, par, q, :], ACT.Identity, bias=dtb[:, q:q + 1]))
                act_steps.wait(act, c, 2 * Q)
                act_steps.link(act, act.activation(ab[:, par], xb[:, par], ACT.Abs))
                act_steps.link(act, act.activation(ab[:, par], ab[:, par], ACT.Exp, scale=-1.0))
                act_steps.inc(act.activation(ab[:, par], ab[:, par], ACT.Ln, bias=1.0))
            in_turn(act, NCH, evac)

        @block.tensor
        def _(pe):
            pe_steps.start(pe)
            pe.wait_ge(consts, 96)

            def work(c, par, half):
                pe_steps.begin(c)
                norm_steps.wait_all(pe, c)
                act_steps.wait_freed(pe, c)

                def turn(src, free):
                    for q in range(Q):
                        free(q)
                        for j in range(J):
                            mm = pe.transpose(tp[:, par, q, j * P:(j + 1) * P], src[:, par, j, q * P:(q + 1) * P], ident[:])
                    pe_steps.inc(mm)
                proj_steps.wait_freed(pe, c)
                turn(zh, lambda q: None)
                turn(z, lambda q: act_steps.wait(pe, c, q + 1))
                proj_steps.wait(pe, c, Q)
                for i in range(2):
                    for q in range(Q):
                        mm = pe.matmul(tp[:, par, i, :], xp[:, q, i * P:(i + 1) * P], znt[:, par, q, :], start=(q == 0), stop=(q == Q - 1))
                    pe_steps.inc(mm)
                proj_steps.wait(pe, c, Q + 2)
                for q in range(Q):
                    pe_steps.inc(pe.matmul(tp[:, par, q, :], dtw[:, q * P:(q + 1) * P], dl[:], start=True, stop=True))
            in_turn(pe, NCH, work)


def scan_phase(nc, B, L, a_log, d_diag, ident_d, dt_s, v_s, z_s, bc_s, y_s):
    NS = a_log.shape[2]
    Q = a_log.shape[1]
    KC = L // T
    NCH = B * KC
    TA = T + 1
    PER = Q + 2
    with ExitStack() as ctx:
        sb = lambda n, s: ctx.enter_context(nc.sbuf_tensor("scan_" + n, s, F32))
        ps = lambda n, s: ctx.enter_context(nc.psum_tensor("scan_" + n, s, F32))
        sem = lambda n: ctx.enter_context(nc.semaphore("scan_" + n))
        y_ps = ps("y", [P, Q, T])
        bb_ps = ps("bb", [P, 2, T])
        dt = sb("dt", [P, 2, Q, T]); v = sb("v", [P, 2, Q, T]); z = sb("z", [P, 2, Q, T])
        bt = sb("bt", [P, 2, T]); bm = sb("bm", [P, 2, T])
        a = sb("a", [P, 2, Q, TA]); u = sb("u", [P, 2, Q, TA]); h = sb("h", [P, 2, Q, TA]); hc = sb("hc", [P, 2, Q, T])
        cb = sb("cb", [P, NS, P]); yo = sb("yo", [P, 1, Q, T])
        carry = sb("carry", [P, NS, Q]); keep = sb("keep", [P, NCH])
        alog = sb("alog", [P, Q, NS]); aexp = sb("aexp", [P, Q, NS]); aneg = sb("aneg", [P, Q, NS])
        ident = sb("ident", [P, P]); ones = sb("ones", [P, P]); dd = sb("dd", [P, Q, P]); dcol = sb("dcol", [P, Q])
        consts = sem("consts"); aneg_ready = sem("aneg_ready"); dd_ready = sem("dd_ready"); filled = sem("filled"); y_zeroed = sem("y_zeroed")
        ticks = {e: sem("ticks_" + e) for e in ("pool", "dve", "act")}
        dt_in, v_in, z_in, bt_in = ([sem(f"{n}{i}") for i in range(2)] for n in ("dt_in", "v_in", "z_in", "bt_in"))
        y_out = sem("y_out"); cb_in = sem("cb_in")
        dt_free = sem("dt_free"); v_free = sem("v_free"); z_free = sem("z_free")
        bm_ready = sem("bm_ready")
        bb_ready = sem("bb_ready")
        a_ready = sem("a_ready")
        u_ready = sem("u_ready")
        h_ready = sem("h_ready")
        hc_ready = sem("hc_ready")
        hc_used = sem("hc_used")
        y_done = sem("y_done")
        y_copied = sem("y_copied")
        block = ctx.enter_context(nc.Block())

        def by_chunk(eng, chunk):
            if NCH > 2:
                with eng.Fori(0, NCH // 2 - 1) as p:
                    for par in range(2):
                        chunk(p * 2 + par, par, p, False)
            for par in range(2):
                chunk(NCH - 2 + par, par, NCH // 2 - 1, par == 1)

        @block.sync
        def _(sp):
            for dst, src in ((alog, a_log), (ident, ident_d), (dcol, d_diag)):
                sp.dma_start(dst[:], src).then_inc(consts, 16)
            with sp.Fori(0, NCH // 2) as k:
                for par in range(2):
                    c = k * 2 + par
                    sp.wait_ge(dt_free, c + 1)
                    sp.dma_start(bt[:, par, :], bc_s[c]).then_inc(bt_in[par], 16)
                    sp.dma_start(dt[:, par], dt_s[c]).then_inc(dt_in[par], 16)
                    sp.wait_ge(v_free, c + 1)
                    sp.dma_start(v[:, par], v_s[c]).then_inc(v_in[par], 16)
                    sp.wait_ge(z_free, c + 1)
                    sp.dma_start(z[:, par], z_s[c]).then_inc(z_in[par], 16)

        @block.gpsimd
        def _(pool):
            pool.sem_inc(hc_ready, 2)
            with pool.Fori(0, B) as b:
                pool.wait_ge(hc_ready, b * (KC * NS) + 2)
                hold(pool, ticks["pool"])
                pool.dma_start(cb[:], bc_s[b * KC, P // 2:P // 2 + NS, 0:P].partition_broadcast(P)).then_inc(cb_in, 16)
                pool.wait_ge(cb_in, (b + 1) * 16)
                hold(pool, ticks["pool"])
                with pool.Fori(0, KC) as k:
                    with pool.Fori(0, NS // 2) as m:
                        for i in range(2):
                            n = m * 2 + i
                            g = (b * KC + k) * NS + n
                            pool.wait_ge(h_ready, g + 3)
                            pool.wait_ge(hc_used, g + 1)
                            pool.tensor_tensor(
                                hc[:, i].rearrange("p q (r j) -> p q r j", j=P),
                                h[:, i, :, 1:TA].rearrange("p q (r j) -> p q r j", j=P),
                                cb[:, bass.ds(n, 1), :].rearrange("p o (x j) -> p o x j", x=1).broadcast_to([P, Q, T // P, P]), ALU.mult
                            ).then_inc(hc_ready, 1)

        @block.scalar
        def _(act):
            act.sem_inc(dt_free, 2)
            act.sem_inc(a_ready, 2 * PER)
            act.sem_inc(y_out, 16)
            act.wait_ge(consts, 48)
            act.activation(aexp[:], alog[:], ACT.Exp).then_inc(aneg_ready, 1)
            act.wait_ge(aneg_ready, 1)
            act.mul(aneg[:], aexp[:], -1.0).then_inc(aneg_ready, 1)
            act.wait_ge(aneg_ready, 2)
            act.wait_ge(filled, 7)

            def mask_row(c, par, n, i):
                act.wait_ge(bb_ready, c * NS + n + 1)
                act.activation(bm[:, i, :], bt[:, par, :], ACT.Identity, scale=ident[:, bass.ds(n, 1)]).then_inc(bm_ready, 1)

            def copy_out(c):
                act.wait_ge(y_out, (c + 1) * 16)
                act.wait_ge(y_zeroed, Q)
                for q in range(Q):
                    if q < Q - 1:
                        act.wait_ge(y_done, c * (Q - 1) + q + 1)
                    else:
                        act.wait_ge(hc_used, c * NS + 2)
                    act.copy(yo[:, 0, q, :], y_ps[:, q, :]).then_inc(y_copied, 1)
                act.wait_ge(y_copied, (c + 1) * Q)
                act.dma_start(y_s[c], yo[:, 0]).then_inc(y_out, 16)

            def chunk(c, par, p, last):
                act.wait_ge(dt_in[par], (p + 1) * 16)

                def step(n, i, kept, ahead):
                    g = c * NS + n
                    act.wait_ge(h_ready, g + 1)
                    act.copy(carry[:, bass.ds(kept, 1), :].rearrange("p o q -> p (o q)"), h[:, i, :, T]).then_inc(a_ready, 1)
                    for q in range(Q):
                        if q == 2 and ahead:
                            mask_row(*ahead, i)
                        act.activation(a[:, i, q, 1:TA], dt[:, par, q, :], ACT.Exp, scale=aneg[:, q, bass.ds(n, 1)]).then_inc(a_ready, 1)
                    act.wait_ge(a_ready, (g + 1) * PER)
                    hold(act, ticks["act"])
                    act.activation(u[:, i, :, 0], carry[:, bass.ds(n, 1), :].rearrange("p o q -> p (o q)"), ACT.Identity, scale=keep[:, bass.ds(c, 1)]).then_inc(a_ready, 1)

                for n in range(4):
                    step(n, n % 2, (n - 2) % NS, (c, par, n + 2))
                    if n == 2:
                        copy_out(c)
                with act.Fori(2, NS // 2 - 1) as m:
                    for i in range(2):
                        step(m * 2 + i, i, m * 2 + i - 2, (c, par, m * 2 + i + 2))
                if not last:
                    act.wait_ge(bt_in[1 - par], (p + 1 + par) * 16)
                for i in range(2):
                    step(NS - 2 + i, i, NS - 4 + i, None if last else (c + 1, 1 - par, i))
                act.wait_ge(a_ready, ((c + 1) * NS + 2) * PER)
                act.sem_inc(dt_free, 1)

            act.wait_ge(bt_in[0], 16)
            mask_row(0, 0, 0, 0)
            mask_row(0, 0, 1, 1)
            by_chunk(act, chunk)
            copy_out(NCH)
            act.wait_ge(y_out, 16 * (NCH + 2))

        @block.tensor
        def _(pe):
            pe.sem_inc(bb_ready, 2)
            pe.sem_inc(hc_used, 2)
            pe.sem_inc(z_free, 2)
            pe.sem_inc(y_done, Q - 1)
            pe.wait_ge(dd_ready, Q)
            pe.wait_ge(filled, 7)
            for q in range(Q):
                pe.matmul(y_ps[:, q, :], ones[:], u[:, 0, q, 1:TA], start=True, stop=True).then_inc(y_zeroed, 1)

            def spread(g, i):
                pe.wait_ge(bm_ready, g + 1)
                pe.wait_ge(u_ready, g + 1)
                pe.matmul(bb_ps[:, i, :], ones[:], bm[:, i, :], start=True, stop=True).then_inc(bb_ready, 1)

            def chunk(c, par, p, last):
                def reduce(n, i):
                    pe.wait_ge(hc_ready, c * NS + n + 3)
                    for q in range(Q):
                        mm = pe.matmul(y_ps[:, q, :], ident[:], hc[:, i, q, :], start=False, stop=True, skip_group_check=True)
                    mm.then_inc(hc_used, 1)

                spread(c * NS + 3, 1)
                pe.wait_ge(hc_ready, c * NS + 3)
                for q in range(Q):
                    pe.wait_ge(y_copied, c * Q + q + 1)
                    mm = pe.matmul(y_ps[:, q, :], ident[:], hc[:, 0, q, :], start=True, stop=True)
                mm.then_inc(hc_used, 1)
                spread(c * NS + 4, 0)
                reduce(1, 1)
                with pe.Fori(1, (NS - 4) // 2) as m:
                    for i in range(2):
                        spread(c * NS + m * 2 + 3 + i, (1 + i) % 2)
                        reduce(m * 2 + i, i)
                pe.wait_ge(z_in[par], (p + 1) * 16)
                for q in range(Q):
                    mm = pe.matmul(y_ps[:, q, :], dd[:, q, :], z[:, par, q, :], start=False, stop=True, skip_group_check=True)
                mm.then_inc(z_free, 1)
                for n in range(NS - 4, NS):
                    if n == NS - 4 or not last:
                        spread(c * NS + n + 3, (n + 1) % 2)
                    if n < NS - 1:
                        reduce(n, n % 2)
                pe.wait_ge(hc_ready, (c + 1) * NS + 2)
                for q in range(Q):
                    pe.matmul(y_ps[:, q, :], ident[:], hc[:, 1, q, :], start=False, stop=True, skip_group_check=True).then_inc(y_done if q < Q - 1 else hc_used, 1)

            for n in range(3):
                spread(n, n % 2)
            by_chunk(pe, chunk)

        @block.vector
        def _(dve):
            dve.sem_inc(u_ready, 2)
            dve.sem_inc(h_ready, 2)
            dve.sem_inc(v_free, 2)
            dve.memset(u[:, 0], 0.0).then_inc(filled, 1)
            dve.memset(ones[:], 1.0).then_inc(filled, 1)
            dve.memset(a[:, :, :, 0:1], 0.0).then_inc(filled, 1)
            dve.memset(h[:, :, :, T:TA], 0.0).then_inc(filled, 1)
            dve.memset(carry[:], 0.0).then_inc(filled, 1)
            dve.memset(keep[:], 1.0).then_inc(filled, 1)
            dve.wait_ge(filled, 6)
            dve.memset(keep[:, 0:NCH:KC], 0.0).then_inc(filled, 1)
            dve.wait_ge(filled, 7)
            dve.wait_ge(consts, 48)
            for q in range(Q):
                dve.tensor_scalar(dd[:, q, :], ident[:], dcol[:, q:q + 1], None, ALU.mult).then_inc(dd_ready, 1)
            dve.wait_ge(y_zeroed, Q)

            def inputs(g, par, i):
                dve.wait_ge(bb_ready, g + 3)
                dve.wait_ge(h_ready, g + 1)
                dve.tensor_tensor(u[:, i, :, 1:TA], v[:, par], bb_ps[:, i:i + 1, :].broadcast_to([P, Q, T]), ALU.mult).then_inc(u_ready, 1)

            def chunk(c, par, p, last):
                def scans(n, i):
                    g = c * NS + n
                    dve.wait_ge(u_ready, g + 3)
                    dve.wait_ge(hc_ready, g + 1)
                    dve.wait_ge(a_ready, (g + 3) * PER)
                    flat = lambda t: t[:, i].rearrange("p q t -> p (q t)")
                    dve.tensor_tensor_scan(flat(h), flat(a), flat(u), 0.0, ALU.mult, ALU.add).then_inc(h_ready, 1)

                with dve.Fori(0, NS // 2 - 1) as m:
                    for i in range(2):
                        scans(m * 2 + i, i)
                        inputs(c * NS + m * 2 + 2 + i, par, i)
                dve.wait_ge(u_ready, c * NS + NS + 2)
                dve.sem_inc(v_free, 1)
                if not last:
                    dve.wait_ge(v_in[1 - par], (p + 1 + par) * 16)
                for i in range(2):
                    scans(NS - 2 + i, i)
                    if not last:
                        inputs((c + 1) * NS + i, 1 - par, i)

            dve.wait_ge(v_in[0], 16)
            inputs(0, 0, 0)
            inputs(1, 0, 1)
            by_chunk(dve, chunk)


def mid_phase(nc, NCH, D, x_d, y_s, wout_d, w0_d, b0_d, ns_d, nb_d, wx_d, ww_d, bw_d, wk_d, wr_d, wv_d, ident_d, x2_s, a_s, k_s, r_s, v_s):
    Q = D // P
    J = T // P
    with ExitStack() as ctx:
        sb = lambda n, s: ctx.enter_context(nc.sbuf_tensor("mid_" + n, s, F32))
        ps = lambda n, s: ctx.enter_context(nc.psum_tensor("mid_" + n, s, F32))
        sem = lambda n: ctx.enter_context(nc.semaphore("mid_" + n))
        pa = ps("pa", [P, Q, T]); pb = ps("pb", [P, Q, T])
        yt = sb("yt", [P, 2, Q, T]); x = sb("x", [P, 2, J, D]); x2 = sb("x2", [P, 2, J, D]); h = sb("h", [P, J, D])
        ht = sb("ht", [P, Q, T]); xnt = sb("xnt", [P, 2, Q, T]); wxw = sb("wxw", [P, Q, D])
        at = sb("at", [P, Q, T]); kt = sb("kt", [P, Q, T]); rt = sb("rt", [P, Q, T]); vv = sb("vv", [P, J, D])
        w = {n: sb(n, [P, Q, D]) for n in ("wout", "w0", "wx", "ww", "wk", "wr", "wv")}
        b0 = sb("b0", [P, 1, D]); ident = sb("ident", [P, P])
        ns = sb("ns", [P, Q]); nb = sb("nb", [P, Q]); bw = sb("bw", [P, Q]); bwn = sb("bwn", [P, Q])
        st = sb("st", [P, J, 6]); mv = sb("mv", [P, J, 2]); ve = sb("ve", [P, J])
        half_neg = sb("half_neg", [P, J]); r0 = sb("r0", [P, J]); rr = sb("rr", [P, J]); tmp = sb("tmp", [P, J])
        consts = sem("consts"); ticks_dve = sem("ticks_dve"); half_ready = sem("half_ready"); bwn_ready = sem("bwn_ready")
        y_in = [sem(f"y_in{i}") for i in range(2)]
        x_in = [sem(f"x_in{i}") for i in range(2)]
        x2_out = [sem(f"x2_out{i}") for i in range(2)]
        outs = sem("outs")
        norm_steps = Count(sem("norm_steps"), 2 * J + 3 * NORM_DVE)
        root_steps = Count(sem("root_steps"), 4)
        turn_steps = Count(sem("turn_steps"), 2 * Q)
        ffn_steps = Count(sem("ffn_steps"), 2 * J + 2)
        proj_steps = Count(sem("proj_steps"), 4 * Q)
        actp_steps = Count(sem("actp_steps"), 2 * Q)
        fold_in = sem("fold_in"); folded = sem("folded"); wxw_ready = sem("wxw_ready")
        dvep_steps = Count(sem("dvep_steps"), 2 * Q)
        CONSTS = 10
        S_X1, S_H, S_X2 = J, J + NORM_DVE, 2 * J + NORM_DVE
        xv = x_d.rearrange("(c j p) d -> c p j d", j=J, p=P)
        x2v = x2_s.rearrange("(c j p) d -> c p j d", j=J, p=P)
        vv_out = v_s.rearrange("(c j p) d -> c p j d", j=J, p=P)
        block = ctx.enter_context(nc.Block())

        @block.sync
        def _(sp):
            for dst, src in ((w["wx"], wx_d), (w["ww"], ww_d)):
                sp.dma_start(dst[:], src).then_inc(fold_in, 16)
            loads = [(w["wout"], wout_d), (w["w0"], w0_d), (w["wk"], wk_d), (w["wr"], wr_d), (w["wv"], wv_d),
                     (b0, b0_d.partition_broadcast(P)), (ident, ident_d), (ns, ns_d), (nb, nb_d), (bw, bw_d)]
            for dst, src in loads:
                sp.dma_start(dst[:], src).then_inc(consts, 16)
            for par in range(2):
                sp.sem_inc(x2_out[par], 16)
            sp.sem_inc(outs, 64)

            def load(c, par, half):
                ffn_steps.wait_freed(sp, c)
                sp.dma_start(yt[:, par], y_s[c + 1]).then_inc(y_in[par], 16)
                sp.dma_start(x[:, par], xv[c]).then_inc(x_in[par], 16)

            def store_x2(c, par, half):
                norm_steps.wait(sp, c, S_X2)
                sp.dma_start(x2v[c], x2[:, par]).then_inc(x2_out[par], 16)

            def store(c, par, half):
                actp_steps.wait(sp, c, Q)
                sp.dma_start(a_s[c], at[:]).then_inc(outs, 16)
                dvep_steps.wait(sp, c, Q)
                sp.dma_start(k_s[c], kt[:]).then_inc(outs, 16)
                actp_steps.wait_all(sp, c)
                sp.dma_start(r_s[c], rt[:]).then_inc(outs, 16)
                dvep_steps.wait_all(sp, c)
                sp.dma_start(vv_out[c], vv[:]).then_inc(outs, 16)
            staggered(sp, NCH, [(2, load), (1, store_x2), (0, store)])
            for par in range(2):
                sp.wait_ge(x2_out[par], 16 * (NCH // 2 + 1))
            sp.wait_ge(outs, 64 * (NCH + 1))

        @block.gpsimd
        def _(pool):
            root_steps.start(pool)
            pool.memset(half_neg[:], -0.5).then_inc(half_ready, 1)
            pool.wait_ge(half_ready, 1)
            pool.wait_ge(consts, CONSTS * 16)

            def roots(c, par, half):
                root_steps.begin(c)
                root_pool(pool, root_steps, norm_steps, c, S_X1 + NORM_VE, r0[:], ve[:], half_neg[:])
                norm_steps.wait(pool, c, S_H)
                root_steps.inc(pool.tensor_tensor(x[:, par], x[:, par], b0[:].broadcast_to([P, J, D]), ALU.add))
                for n in (S_X2, S_X2 + NORM_DVE):
                    root_pool(pool, root_steps, norm_steps, c, n + NORM_VE, r0[:], ve[:], half_neg[:])
            in_turn(pool, NCH, roots)

        @block.vector
        def _(dve):
            norm_steps.start(dve)
            dvep_steps.start(dve)

            def norm(c, n, out, src):
                norm_dve(dve, ticks_dve, norm_steps, root_steps, c, n, out, src, st, mv, ve[:], r0[:], rr[:], tmp[:], J)

            def first_sum(c, par, half):
                norm_steps.begin(c)
                dve.wait_ge(x_in[par], (half + 1) * 16)
                for j in range(J):
                    ffn_steps.wait(dve, c, j + 1)
                    norm_steps.inc(dve.tensor_tensor(x[:, par, j, :], x[:, par, j, :], pa[:, j, :], ALU.add))
                norm_steps.wait(dve, c, S_X1)
                norm(c, 1, h, x[:, par])

            def second_sum(c, par, half):
                dve.wait_ge(x2_out[par], (half + 1) * 16)
                root_steps.wait(dve, c, 2)
                for j in range(J):
                    ffn_steps.wait(dve, c, J + 1 + j + 1)
                    norm_steps.inc(dve.tensor_tensor(x2[:, par, j, :], x[:, par, j, :], pa[:, j, :], ALU.add))

            def more_norms(c, par, half):
                norm_steps.wait(dve, c, S_X2)
                norm(c, 3, h, x2[:, par])
                norm(c, 4, x[:, par], h)

            def keys(c, par, half):
                dvep_steps.begin(c)
                dve.wait_ge(outs, (c + 1) * 64)
                for q in range(Q):
                    proj_steps.wait(dve, c, Q + q + 1)
                    dvep_steps.inc(dve.tensor_copy(kt[:, q, :], pb[:, q, :]))

            def values(c, par, half):
                for j in range(J):
                    proj_steps.wait(dve, c, 3 * Q + j + 1)
                    dvep_steps.inc(dve.tensor_copy(vv[:, j, :], pb[:, j, :]))
            skewed(dve, NCH, [(1, first_sum), (1, second_sum), (0, keys), (1, more_norms), (0, values)])

        @block.scalar
        def _(act):
            turn_steps.start(act)
            actp_steps.start(act)
            act.wait_ge(consts, CONSTS * 16)
            act.mul(bwn[:], bw[:], -1.0).then_inc(bwn_ready, 1)
            act.wait_ge(bwn_ready, 1)
            act.wait_ge(folded, 1)
            act.copy(wxw[:], pa[:]).then_inc(wxw_ready, 1)

            def turned_h(c, par, half):
                turn_steps.begin(c)
                ffn_steps.wait(act, c, J + 1)
                for q in range(Q):
                    turn_steps.inc(act.copy(ht[:, q, :], pa[:, q, :]))

            def decays(c, par, half):
                actp_steps.begin(c)
                act.wait_ge(outs, (c + 1) * 64)
                for q in range(Q):
                    proj_steps.wait(act, c, q + 1)
                    actp_steps.inc(act.activation(at[:, q, :], pb[:, q, :], ACT.Sigmoid, bias=bwn[:, q:q + 1], scale=-1.0))

            def reads(c, par, half):
                for q in range(Q):
                    proj_steps.wait(act, c, 2 * Q + q + 1)
                    actp_steps.inc(act.activation(rt[:, q, :], pb[:, q, :], ACT.Sigmoid))

            def turned_xn(c, par, half):
                proj_steps.wait_freed(act, c)
                ffn_steps.wait_all(act, c)
                for q in range(Q):
                    turn_steps.inc(act.activation(xnt[:, par, q, :], pa[:, q, :], ACT.Identity, bias=nb[:, q:q + 1], scale=ns[:, q:q + 1]))
            skewed(act, NCH, [(0, decays), (1, turned_h), (0, reads), (1, turned_xn)])

        @block.tensor
        def _(pe):
            ffn_steps.start(pe)
            proj_steps.start(pe)
            pe.wait_ge(fold_in, 32)
            for q in range(Q):
                for i in range(Q):
                    mm = pe.matmul(pa[:, q, :], w["wx"][:, i, q * P:(q + 1) * P], w["ww"][:, i, :], start=(i == 0), stop=(i == Q - 1))
            mm.then_inc(folded, 1)
            pe.wait_ge(wxw_ready, 1)
            pe.wait_ge(consts, CONSTS * 16)

            def attn_out(c, par, half):
                ffn_steps.begin(c)
                pe.wait_ge(y_in[par], (half + 1) * 16)
                turn_steps.wait_before(pe, c)
                for j in range(J):
                    for q in range(Q):
                        mm = pe.matmul(pa[:, j, :], yt[:, par, q, j * P:(j + 1) * P], w["wout"][:, q, :], start=(q == 0), stop=(q == Q - 1))
                    ffn_steps.inc(mm)

            def turn(src):
                for q in range(Q):
                    for j in range(J):
                        mm = pe.transpose(pa[:, q, j * P:(j + 1) * P], src[:, j, q * P:(q + 1) * P], ident[:])
                ffn_steps.inc(mm)

            def turn_h(c, par, half):
                norm_steps.wait(pe, c, S_H)
                turn(h)

            def ffn(c, par, half):
                turn_steps.wait(pe, c, Q)
                for j in range(J):
                    for q in range(Q):
                        mm = pe.matmul(pa[:, j, :], ht[:, q, j * P:(j + 1) * P], w["w0"][:, q, :], start=(q == 0), stop=(q == Q - 1))
                    ffn_steps.inc(mm)

            def turn_xn(c, par, half):
                norm_steps.wait_all(pe, c)
                turn(x[:, par])

            def columns(weight, src, free):
                for o in range(Q):
                    free(o)
                    for q in range(Q):
                        mm = pe.matmul(pb[:, o, :], weight[:, q, o * P:(o + 1) * P], src[:, q, :], start=(q == 0), stop=(q == Q - 1))
                    proj_steps.inc(mm)

            def decay(c, par, half):
                proj_steps.begin(c)
                turn_steps.wait_all(pe, c)
                dvep_steps.wait_before(pe, c)
                columns(wxw, xnt[:, par], lambda o: None)

            def keys(c, par, half):
                columns(w["wk"], xnt[:, par], lambda o: actp_steps.wait(pe, c, o + 1))

            def reads(c, par, half):
                columns(w["wr"], xnt[:, par], lambda o: dvep_steps.wait(pe, c, o + 1))

            def values(c, par, rows):
                for j in rows:
                    actp_steps.wait(pe, c, Q + j + 1)
                    for q in range(Q):
                        mm = pe.matmul(pb[:, j, :], xnt[:, par, q, j * P:(j + 1) * P], w["wv"][:, q, :], start=(q == 0), stop=(q == Q - 1))
                    proj_steps.inc(mm)

            def values_early(c, par, half):
                values(c, par, range(J // 2))

            def values_late(c, par, half):
                values(c, par, range(J // 2, J))
            skewed(pe, NCH, [(1, attn_out), (0, decay), (1, turn_h), (0, keys), (1, ffn), (0, reads), (0, values_early), (1, turn_xn), (0, values_late)])


SUB = 8
BIG = 3.0e38


def core_phase(nc, D, H, L, a_s, k_s, r_s, v_s, x2_s, wo_d, gam_d, bet_d, slopes_d, crow_d, trow_d, mask_d, hmask_d, ident_d, x3_s, oh_out, xs_out, ext_out):
    B = 2
    ITEMS = B * L // P
    Q = D // P
    NI = P // SUB
    W = SUB + 1
    LEVELS = (NI - 1).bit_length()
    pairs = [NI >> (l + 1) for l in range(LEVELS)]
    E_AT = [Q * sum(pairs[:l]) for l in range(LEVELS)]
    HP = P // 2
    E = D // H
    TPC = T // P
    with ExitStack() as ctx:
        sb = lambda n, s: ctx.enter_context(nc.sbuf_tensor("core_" + n, s, F32))
        ps = lambda n, s: ctx.enter_context(nc.psum_tensor("core_" + n, s, F32))
        sem = lambda n: ctx.enter_context(nc.semaphore("core_" + n))
        sc_ps = ps("sc_ps", [P, H, T // H]); at_ps = ps("at_ps", [P, 2, Q // 2, 2, P]); o_ps = ps("o_ps", [P, 2, T // P, P])
        kt_ps = ps("kt_ps", [P, Q, P]); su_ps = ps("su_ps", [P, Q, P]); y_ps = ps("y_ps", [P, D])
        a = sb("a", [P, 2, Q, P]); k = sb("k", [P, 2, Q, P]); r = sb("r", [P, 2, Q, P]); v = sb("v", [P, 2, D]); x = sb("x", [P, 2, D])
        rr = sb("rr", [P, SUB, Q * NI, W]); first = sb("first", [P, 2, Q * NI, W]); rk = sb("rk", [P, W, Q, P])
        ee = sb("ee", [P, 2, E_AT[-1] + Q, 4]); total = sb("total", [P, 2, Q, 1])
        kl = sb("kl", [P, 2, LEVELS, Q, P]); ql = sb("ql", [P, 2, LEVELS, Q, P])
        kz = sb("kz", [P, 2, 2, Q, P]); qb = sb("qb", [P, 2, LEVELS, Q, 2, HP])
        af = sb("af", [P, H, P]); ats = sb("ats", [P, 2, Q // 2, 2, P]); k8t = sb("k8t", [P, Q, P])
        ot = sb("ot", [P, Q, P]); s = sb("s", [P, 2, Q, P]); s1 = sb("s1", [P, Q, P])
        x3 = sb("x3", [P, 2, D]); z = sb("z", [P, 1, D]); zh = sb("zh", [P, 1, D]); xf = sb("xf", [P, D]); sg = sb("sg", [P, D]); pr = sb("pr", [P, D])
        wo = sb("wo", [P, Q, D]); gam = sb("gam", [P, D]); bet = sb("bet", [P, D]); sig = sb("sig", [P, D])
        NT = D // 8
        NCL = NT // 8
        crow = sb("crow", [P, NCL]); trow = sb("trow", [P, NT])
        mask = sb("mask", [P, P]); hmask = sb("hmask", [P, P]); ident = sb("ident", [P, P])
        st = sb("st", [P, 1, 6]); mv = sb("mv", [P, 1, 2]); ve = sb("ve", [P, 1]); half_neg = sb("half_neg", [P, 1]); r0 = sb("r0", [P, 1]); rt = sb("rt", [P, 1]); tmp = sb("tmp", [P, 1])
        ts = sb("ts", [P, NT]); cs = sb("cs", [P, NCL]); key = sb("key", [P, NT]); kmax = sb("kmax", [P, 1]); pen = sb("pen", [P, NT]); sel = sb("sel", [P, 2, NT])
        mm2 = sb("mm2", [P, 2])
        oh = sb("oh", [P, ITEMS, NT]); xs = sb("xs", [P, ITEMS, 8]); xsd = sb("xsd", [P, 8]); ext = sb("ext", [P, 2, NT])
        consts = sem("consts"); ticks_dve = sem("ticks_dve"); ticks_pool = sem("ticks_pool"); ticks_sp = sem("ticks_sp"); pool_ready = sem("pool_ready"); slope_sum = sem("slope_sum"); slope_signs = sem("slope_signs"); on_diagonal = sem("on_diagonal"); sig_spread = sem("sig_spread"); sig_ready = sem("sig_ready"); zeroed = sem("zeroed")
        ins_a = [sem(f"ins_a{i}") for i in range(2)]
        ins_b = [sem(f"ins_b{i}") for i in range(2)]
        x3_out = [sem(f"x3_out{i}") for i in range(2)]
        final = sem("final"); kmax_ready = sem("kmax_ready")
        chain = Count(sem("chain"), 1 + 2 * SUB)
        diagonal = Count(sem("diagonal"), 1)
        spread = Count(sem("spread"), 1)
        after = Count(sem("after"), 4 + 2 * NORM_DVE + 14)
        pool_a = Count(sem("pool_a"), LEVELS + 2 * LEVELS)
        act_q = Count(sem("act_q"), 1 + LEVELS)
        sign = Count(sem("sign"), 1)
        A_TOTAL = LEVELS
        pool_b = Count(sem("pool_b"), 2 + 5)
        act_a = Count(sem("act_a"), 5)
        pe_a = Count(sem("pe_a"), 1)
        pe_b = Count(sem("pe_b"), 7)
        S_X3 = 4
        S_N1, S_N2 = 4 + NORM_DVE, 4 + 2 * NORM_DVE

        GRID = slopes_d.shape[0] // D
        slopes = sb("slopes", [P, Q, GRID]); slope_sign = sb("slope_sign", [P, Q])
        ones, signs_on_diagonal = pr[:, 0:P], sg[:].rearrange("p (j c) -> p j c", c=P)

        def ones_and_decays(par, l):
            return ee[:, par, E_AT[l]:E_AT[l] + Q * pairs[l], :]

        block = ctx.enter_context(nc.Block())

        @block.sync
        def _(sp):
            for dst, src in ((wo, wo_d), (gam, gam_d.partition_broadcast(P)), (bet, bet_d.partition_broadcast(P)), (crow, crow_d), (trow, trow_d), (mask, mask_d),
                             (hmask, hmask_d), (ident, ident_d)):
                sp.dma_start(dst[:], src).then_inc(consts, 16)
            sp.dma_start(slopes[:], slopes_d.rearrange("(p j g) -> p j g", p=P, g=GRID)).then_inc(consts, 16)
            for par in range(2):
                sp.sem_inc(x3_out[par], 16)

            def load_decays(i, par, m):
                c = m // TPC + par * (L // T)
                t = m % TPC
                chain.wait_freed(sp, i)
                hold(sp, ticks_sp)
                pool_a.wait_freed(sp, i)
                hold(sp, ticks_sp)
                for dst, src in ((a, a_s), (k, k_s), (r, r_s)):
                    sp.dma_start(dst[:, par], src[c, :, :, bass.ds(t * P, P)]).then_inc(ins_a[par], 16)

            def load_rows(i, par, m):
                after.wait_freed(sp, i)
                hold(sp, ticks_sp)
                pe_b.wait_freed(sp, i)
                hold(sp, ticks_sp)
                sp.dma_start(v[:, par], v_s[bass.ds((m + par * (L // P)) * P, P), :]).then_inc(ins_b[par], 16)
                sp.dma_start(x[:, par], x2_s[bass.ds((m + par * (L // P)) * P, P), :]).then_inc(ins_b[par], 16)

            def store(i, par, m):
                pool_b.wait(sp, i, 5)
                hold(sp, ticks_sp)
                sp.dma_start(x3_s[bass.ds((m + par * (L // P)) * P, P), :], x3[:, par]).then_inc(x3_out[par], 16)
            staggered(sp, ITEMS, [(2, load_decays), (1, load_rows), (0, store)])
            after.wait_all(sp, ITEMS - 1)
            sp.dma_start(oh_out, oh[:]).then_inc(final, 16)
            sp.dma_start(xs_out, xs[:]).then_inc(final, 16)
            sp.dma_start(ext_out, ext[:]).then_inc(final, 16)
            sp.wait_ge(final, 48)
            for par in range(2):
                sp.wait_ge(x3_out[par], 16 * (ITEMS // 2 + 1))

        @block.gpsimd
        def _(pool):
            pool_a.start(pool)
            pool_b.start(pool)
            pool.memset(half_neg[:], -0.5).then_inc(pool_ready, 1)
            pool.wait_ge(pool_ready, 1)
            pool.wait_ge(zeroed, 8)
            pool.wait_ge(consts, 144)
            pool.wait_ge(sig_ready, 1)

            def keys(i, par, m):
                pool_a.begin(i)
                pe_b.wait_freed(pool, i)
                hold(pool, ticks_pool)
                chain.wait_all(pool, i)
                for l in range(LEVELS):
                    both = ones_and_decays(par, l)
                    if l + 1 < LEVELS:
                        both = both.rearrange("p (c e) w -> p c e w", e=2)
                        dst = ones_and_decays(par, l + 1)[:, :, 1:3]
                        pool_a.link(pool, pool.tensor_tensor(dst, both[:, :, :, 1], both[:, :, :, 2], ALU.mult))
                    else:
                        pool_a.link(pool, pool.tensor_tensor(total[:, par], both[:, :, 1:2], both[:, :, 2:3], ALU.mult))
                for l in range(LEVELS):
                    n = SUB << l
                    shape = [P, Q * pairs[l], 2, n]
                    e = ones_and_decays(par, l)
                    cut = lambda t: t.rearrange("p q (c e n) -> p (q c) e n", e=2, n=n)
                    key_in = cut(rk[:, SUB] if l == 0 else kl[:, par, l - 1])
                    read_in = first[:, par, :, 0:SUB].rearrange("p (c e) n -> p c e n", e=2) if l == 0 else cut(ql[:, par, l - 1])
                    pool_a.inc(pool.tensor_tensor(cut(kl[:, par, l]), key_in, e[:, :, 2:4].rearrange("p c (e n) -> p c e n", n=1).broadcast_to(shape), ALU.mult))
                    pool_a.link(pool, pool.tensor_tensor(cut(ql[:, par, l]), read_in, e[:, :, 0:2].rearrange("p c (e n) -> p c e n", n=1).broadcast_to(shape), ALU.mult))

            def route(i, par, m):
                pool_b.begin(i)
                for n in (S_X3, S_N1):
                    root_pool(pool, pool_b, after, i, n + NORM_VE, r0[:], ve[:], half_neg[:])
                after.wait(pool, i, S_N2)
                pool_b.link(pool, pool.tensor_tensor(xf[:], zh[:, 0], gam[:], ALU.mult))
                pool_b.inc(pool.tensor_tensor(xf[:], xf[:], bet[:], ALU.add))
                pool_b.inc(pool.tensor_tensor(x3[:, par], x3[:, par], z[:, 0], ALU.add))
                sign.wait_all(pool, i)
                pool_b.inc(pool.tensor_tensor(pr[:], sg[:], sig[:], ALU.mult))
                after.wait(pool, i, S_N2 + 6)
                pool_b.inc(pool.tensor_tensor(pr[:].rearrange("p (n e) -> p n e", e=8), xf[:].rearrange("p (n e) -> p n e", e=8),
                                              oh[:, bass.ds(par * (L // P) + m, 1), :].rearrange("p o (n e) -> p (o n) e", e=1).broadcast_to([P, NT, 8]), ALU.mult))
            staggered(pool, ITEMS, [(0, route), (2, keys)])

        @block.vector
        def _(dve):
            chain.start(dve)
            spread.start(dve)
            after.start(dve)
            dve.memset(kz[:], 0.0).then_inc(zeroed, 1)
            dve.memset(rk[:], 0.0).then_inc(zeroed, 1)
            dve.memset(s[:], 0.0).then_inc(zeroed, 1)
            dve.memset(ext[:], -BIG).then_inc(zeroed, 1)
            dve.memset(qb[:], 0.0).then_inc(zeroed, 1)
            dve.memset(ee[:], 1.0).then_inc(zeroed, 1)
            dve.memset(rr[:, SUB - 1, :, SUB:W], 1.0).then_inc(zeroed, 1)
            dve.memset(ones, 1.0).then_inc(zeroed, 1)
            dve.wait_ge(zeroed, 8)
            dve.wait_ge(consts, 144)
            dve.tensor_reduce(slope_sign[:], slopes[:], AX.X, ALU.add).then_inc(slope_sum, 1)
            dve.wait_ge(slope_signs, 1)
            for j in range(Q):
                last = dve.tensor_scalar(signs_on_diagonal[:, j, :], ident[:], slope_sign[:, j:j + 1], None, ALU.mult)
            last.then_inc(on_diagonal, 1)

            def decays(i, par, m):
                chain.begin(i)
                dve.wait_ge(ins_a[par], (m + 1) * 48)
                pool_a.wait_freed(dve, i)
                act_q.wait_freed(dve, i)
                chain.wait_before(dve, i)
                pe_a.wait_before(dve, i)
                pool_a.wait(dve, i - 1, A_TOTAL + 1)
                act_q.wait(dve, i - 1, 1)
                av = a[:, par].rearrange("p q (i t) -> p (q i) t", t=SUB)
                kv = k[:, par].rearrange("p q (i t) -> p t (q i)", t=SUB)
                diagonal.wait_all(dve, i)
                for j in range(SUB - 1, -1, -1):
                    decayed = chain.inc(dve.tensor_tensor((rr[:, j - 1] if j else first[:, par])[:, :, j:W], rr[:, j, :, j:W], av[:, :, j:j + 1].broadcast_to([P, Q * NI, W - j]), ALU.mult))
                    chain.inc(dve.tensor_tensor(rk[:, j:W].rearrange("p t q (i j) -> p t (q i) j", j=SUB)[:, :, :, j],
                                                rr[:, j, :, j:W].rearrange("p c w -> p w c"), kv[:, j:j + 1].broadcast_to([P, W - j, Q * NI]), ALU.mult))
                    chain.wait(dve, i, decayed)
                chain.inc(dve.tensor_copy(ones_and_decays(par, 0)[:, :, 1:3], first[:, par, :, SUB].rearrange("p (c e) -> p c e", e=2)))

            def spread_scores(i, par, m):
                spread.begin(i)
                pe_a.wait_all(dve, i)
                pe_b.wait(dve, i - 1, 1)
                shape = [P, NI, SUB]
                for h in range(H):
                    last = dve.tensor_tensor(af[:, h].rearrange("p (i t) -> p i t", t=SUB), sc_ps[:, h:h + 1, 0:SUB].broadcast_to(shape),
                                             mask[:].rearrange("p (i t) -> p i t", t=SUB), ALU.mult)
                spread.inc(last)

            def state(i, par, m):
                after.begin(i)
                pe_b.wait(dve, i, 6)
                after.inc(dve.tensor_tensor(s1[:], su_ps[:], hmask[:].rearrange("p (o e) -> p o e", o=1).broadcast_to([P, Q, P]), ALU.mult))
                after.link(dve, dve.tensor_tensor(s[:, par], s[:, par], total[:, par].broadcast_to([P, Q, P]), ALU.mult))
                after.inc(dve.tensor_tensor(s[:, par], s[:, par], s1[:], ALU.add))
                pe_b.wait_all(dve, i)
                dve.wait_ge(ins_b[par], (m + 1) * 32)
                dve.wait_ge(x3_out[par], (m + 1) * 16)
                after.link(dve, dve.tensor_tensor(x3[:, par], x[:, par], y_ps[:], ALU.add))

            def norms(i, par, m):
                norm_dve(dve, ticks_dve, after, pool_b, i, 1, z, x3[:, par:par + 1], st, mv, ve[:], r0[:], rt[:], tmp[:], 1)
                norm_dve(dve, ticks_dve, after, pool_b, i, 2, zh, z, st, mv, ve[:], r0[:], rt[:], tmp[:], 1)

            def route(i, par, m):
                pool_b.wait(dve, i, 6)
                after.link(dve, dve.tensor_reduce(ts[:], pr[:].rearrange("p (n e) -> p n e", e=8), AX.X, ALU.add))
                after.link(dve, dve.tensor_reduce(cs[:], ts[:].rearrange("p (n e) -> p n e", e=8), AX.X, ALU.add))
                after.inc(dve.scalar_tensor_tensor(out=key[:], in0=ts[:], scalar=64.0, in1=trow[:], op0=ALU.mult, op1=ALU.add))
                after.link(dve, dve.scalar_tensor_tensor(out=cs[:], in0=cs[:], scalar=32768.0, in1=crow[:], op0=ALU.mult, op1=ALU.add))
                kv = key[:].rearrange("p (n e) -> p n e", e=8)
                after.link(dve, dve.tensor_tensor(kv, kv, cs[:].rearrange("p (n e) -> p n e", e=1).broadcast_to([P, NCL, 8]), ALU.add))
                dve.tensor_reduce(kmax[:], key[:], AX.X, ALU.max).then_inc(kmax_ready, 1)
                dve.wait_ge(kmax_ready, i + 1)
                after.link(dve, dve.tensor_scalar(oh[:, bass.ds(par * (L // P) + m, 1), :].rearrange("p o n -> p (o n)"), key[:], kmax[:, 0:1], None, ALU.is_equal))
                ohi = oh[:, bass.ds(par * (L // P) + m, 1), :].rearrange("p o n -> p (o n)")
                after.inc(dve.tensor_scalar(pen[:], ohi, -BIG, BIG, ALU.mult, ALU.add))
                pool_b.wait_all(dve, i)
                xsi = xsd[:]
                after.link(dve, dve.tensor_reduce(xsi, pr[:].rearrange("p (n e) -> p e n", e=8), AX.X, ALU.add))
                after.inc(dve.tensor_scalar(xs[:, bass.ds(par * (L // P) + m, 1), :].rearrange("p o n -> p (o n)"), xsi, 1.0, None, ALU.mult))
                after.inc(dve.tensor_reduce(mm2[:, 0:1], xsi, AX.X, ALU.max))
                after.link(dve, dve.tensor_reduce(mm2[:, 1:2], xsi, AX.X, ALU.min, negate=True))
                for e in range(2):
                    last = dve.scalar_tensor_tensor(out=sel[:, e, :], in0=ohi, scalar=mm2[:, e:e + 1], in1=pen[:], op0=ALU.mult, op1=ALU.subtract)
                    after.inc(last)
                after.wait(dve, i, after.n)
                after.link(dve, dve.tensor_tensor(ext[:], ext[:], sel[:], ALU.max))
            staggered(dve, ITEMS, [(0, state), (1, spread_scores), (0, norms), (2, decays), (0, route)])

        @block.scalar
        def _(act):
            act_a.start(act)
            act.wait_ge(slope_sum, 1)
            act.activation(slope_sign[:], slope_sign[:], ACT.Sign, scale=1.0 / GRID).then_inc(slope_signs, 1)
            act.wait_ge(sig_spread, 1)
            act.copy(sig[:].rearrange("p (c j) -> p j c", j=Q), y_ps[:].rearrange("p (j c) -> p j c", j=Q)).then_inc(sig_ready, 1)

            act_q.start(act)
            diagonal.start(act)
            sign.start(act)
            act.wait_ge(zeroed, 8)

            def own_reads(i, par, m):
                diagonal.begin(i)
                chain.wait_before(act, i)
                act.wait_ge(ins_a[par], (m + 1) * 48)
                rv = r[:, par].rearrange("p q (i t) -> p (q i) t", t=SUB)
                for j in range(SUB):
                    last = act.copy(rr[:, j, :, j:j + 1], rv[:, :, j:j + 1])
                diagonal.inc(last)

            def by_head(i, par, m):
                act_q.begin(i)
                pe_b.wait_freed(act, i)
                chain.wait_all(act, i)
                for odd in range(2):
                    cut = lambda t: t.rearrange("p q (c e n) -> p (q c) e n", e=4, n=SUB)[:, :, 2 * odd, :]
                    last = act.copy(cut(kz[:, par, odd]), cut(rk[:, SUB]))
                act_q.inc(last)
                for l in range(LEVELS):
                    n = SUB << l
                    if l == 0:
                        src = first[:, par, :, 0:SUB].rearrange("p (q c e) n -> p q c e n", e=2, q=Q)[:, :, :, 1]
                    else:
                        pool_a.wait(act, i, A_TOTAL + 2 * l)
                        src = ql[:, par, l - 1].rearrange("p q (c e n) -> p q c e n", e=2, n=n)[:, :, :, 1]
                    for h2 in range(2):
                        lo = h2 * E
                        last = act.copy(qb[lo:lo + E, par, l, :, h2, :].rearrange("p q (c n) -> p q c n", n=n), src[lo:lo + E])
                    act_q.inc(last)

            def evac(i, par, m):
                act_a.begin(i)
                for g in range(2):
                    pe_b.wait(act, i, 1 + g)
                    act_a.inc(act.copy(ats[:, g], at_ps[:, g]))
                pe_b.wait(act, i, 3)
                act_a.inc(act.copy(k8t[:], kt_ps[:]))
                for g in range(2):
                    pe_b.wait(act, i, 4 + g)
                    act_a.inc(act.copy(ot[:, g * (Q // 2):(g + 1) * (Q // 2)], o_ps[:, g, 0:Q // 2]))

            def signs(i, par, m):
                sign.begin(i)
                pool_b.wait(act, i, 4)
                sign.inc(act.activation(sg[:], xf[:], ACT.Sign))
            staggered(act, ITEMS, [(2, own_reads), (1, by_head), (1, evac), (0, signs)])

        @block.tensor
        def _(pe):
            pe_a.start(pe)
            pe_b.start(pe)
            pe.wait_ge(consts, 144)
            pe.wait_ge(zeroed, 8)
            pe.wait_ge(on_diagonal, 1)
            for j in range(Q):
                mm = pe.matmul(y_ps[:, j * P:(j + 1) * P], ones, signs_on_diagonal[:, j, :], start=True, stop=True)
            mm.then_inc(sig_spread, 1)

            def scores(i, par, m):
                pe_a.begin(i)
                spread.wait_before(pe, i)
                chain.wait_all(pe, i)
                for t in range(SUB):
                    for q in range(Q):
                        mm = pe.matmul(sc_ps[:, 2 * q:2 * q + 2, t], rk[:, t, q, :], hmask[:, 0:P:E], start=True, stop=True)
                pe_a.inc(mm)

            def attend(i, par, m):
                pe_b.begin(i)
                act_a.wait_before(pe, i)
                spread.wait_all(pe, i)
                for g in range(2):
                    pe.matmul(at_ps[:, g], ident[:], af[:, g * (H // 2):(g + 1) * (H // 2), :], start=True, stop=True)
                act_q.wait_all(pe, i)
                for q in range(Q):
                    to = at_ps[:, q // 2, q % 2]
                    for l in range(LEVELS):
                        n = SUB << l
                        for c in range(pairs[l]):
                            at, reads = 2 * n * c, qb[:, par, l, q, :, n * c:n * (c + 1)]
                            lo, rows = (at, n) if l else (at // 32 * 32, 32)
                            keys = kz[:, par, c % 2, q, lo:lo + rows] if l == 0 else kl[:, par, l - 1, q, lo:lo + rows]
                            mm = pe.matmul(to[lo:lo + rows, :, at + n:at + 2 * n], keys, reads, start=False, stop=True, skip_group_check=True, tile_position=(0, lo))
                    if q % 2:
                        pe_b.inc(mm)
                pool_a.wait_all(pe, i)
                for q in range(Q):
                    mm = pe.transpose(kt_ps[:, q, :], kl[:, par, LEVELS - 1, q, :], ident[:])
                pe_b.inc(mm)
                after.wait_freed(pe, i)
                for q in range(Q):
                    pe.matmul(o_ps[:, q // 2, q % 2, :], s[:, par, q, :], ql[:, par, LEVELS - 1, q, :], start=(q % 2 == 0), stop=True, skip_group_check=True)
                pe.wait_ge(ins_b[par], (m + 1) * 32)
                for q in range(Q):
                    act_a.wait(pe, i, 1 + q // 2)
                    for h2 in range(2):
                        h = 2 * q + h2
                        mm = pe.matmul(o_ps[h2 * E:(h2 + 1) * E, q // 2, q % 2, :], v[:, par, h * E:(h + 1) * E], ats[:, q // 2, q % 2, h2, :], start=False, stop=True, skip_group_check=True)
                    if q % 2:
                        pe_b.inc(mm)
                act_a.wait(pe, i, 3)
                after.wait(pe, i - 1, S_X3)
                for q in range(Q):
                    mm = pe.matmul(su_ps[:, q, :], k8t[:, q, :], v[:, par, q * P:(q + 1) * P], start=True, stop=True)
                pe_b.inc(mm)
                for q in range(Q):
                    act_a.wait(pe, i, 4 + q // 2)
                    mm = pe.matmul(y_ps[:], ot[:, q, :], wo[:, q, :], start=(q == 0), stop=(q == Q - 1))
                pe_b.inc(mm)
            staggered(pe, ITEMS, [(0, attend), (1, scores)])


def final_phase(nc, D, N, x3_s, oh_s, xs_s, ext_s, table_d, grid_d, ident_d, out_d):
    NT, GRID = oh_s.shape[2], 16
    TILES = N // P
    NCH = N // T
    J = T // P
    SL = D // NT
    TW = 2 * SL * GRID + 1
    TOP = 1.0 - 1e-6
    with ExitStack() as ctx:
        sb = lambda n, s: ctx.enter_context(nc.sbuf_tensor("fin_" + n, s, F32))
        ps = lambda n, s: ctx.enter_context(nc.psum_tensor("fin_" + n, s, F32))
        sem = lambda n: ctx.enter_context(nc.semaphore("fin_" + n))
        rows = ps("rows", [P, 2, J, T])
        oh = sb("oh", [P, TILES, NT]); xs = sb("xs", [P, TILES, SL]); ext = sb("ext", [P, 2, NT]); exta = sb("exta", [P, 2, NT])
        pr = sb("pr", [P, TILES, NT]); lim = sb("lim", [P, 2, TILES]); diff = sb("diff", [P, TILES]); rec = sb("rec", [P, TILES])
        u = sb("u", [P, TILES, SL]); u16 = sb("u16", [P, TILES, SL]); gi = sb("gi", [P, TILES, SL])
        ge = sb("ge", [P, TILES, SL, GRID + 1]); hot = sb("hot", [P, TILES, SL, GRID])
        grid = sb("grid", [P, GRID + 1]); table = sb("table", [NT, TW]); ident = sb("ident", [P, P])
        ohc = sb("ohc", [P, 2, J, NT]); oht = sb("oht", [NT, 2, J, P]); wv = sb("wv", [P, J, 2, SL * GRID]); bs = sb("bs", [P, J, 2, SL])
        delta = sb("delta", [P, 2, J, SL]); x = sb("x", [P, 2, J, D]); add = sb("add", [P, 2, J, D])
        consts = sem("consts"); ticks_act = sem("ticks_act"); pre = sem("pre"); ext_all = sem("ext_all")
        x_in = [sem(f"x_in{i}") for i in range(2)]
        out = [sem(f"out{i}") for i in range(2)]
        turned = Count(sem("turned"), 2)
        copied = Count(sem("copied"), 1); staged = Count(sem("staged"), 1)
        spline = Count(sem("spline"), 5)
        summed = Count(sem("summed"), 1)
        placed = Count(sem("placed"), 1)
        xv = x3_s.rearrange("(c j p) d -> c p j d", j=J, p=P)
        ov = out_d.rearrange("(c j p) d -> c p j d", j=J, p=P)
        block = ctx.enter_context(nc.Block())

        @block.sync
        def _(sp):
            for dst, src in ((ext, ext_s), (oh, oh_s), (xs, xs_s), (grid, grid_d), (table, table_d), (ident, ident_d)):
                sp.dma_start(dst[:], src).then_inc(consts, 16)
            for par in range(2):
                sp.sem_inc(out[par], 16)

            def load(c, par, half):
                sp.wait_ge(out[par], (half + 1) * 16)
                sp.dma_start(x[:, par], xv[c]).then_inc(x_in[par], 16)

            def store(c, par, half):
                summed.wait_all(sp, c)
                sp.dma_start(ov[c], x[:, par]).then_inc(out[par], 16)
            skewed(sp, NCH, [(1, load), (0, store)])
            for par in range(2):
                sp.wait_ge(out[par], 16 * (NCH // 2 + 1))

        @block.gpsimd
        def _(pool):
            placed.start(pool)
            pool.wait_ge(consts, 96)
            pool.partition_all_reduce(exta[:].rearrange("p e n -> p (e n)"), ext[:].rearrange("p e n -> p (e n)"), P, bass.bass_isa.ReduceOp.max).then_inc(ext_all, 1)

            def place(c, par, half):
                placed.begin(c)
                spline.wait_all(pool, c)
                summed.wait_freed(pool, c)
                for j in range(J):
                    last = pool.tensor_tensor(add[:, par, j].rearrange("p (n e) -> p n e", e=SL), oh[:, bass.ds(c * J + j, 1), :].rearrange("p o (n e) -> p (o n) e", e=1).broadcast_to([P, NT, SL]),
                                              delta[:, par, j:j + 1, :].broadcast_to([P, NT, SL]), ALU.mult)
                placed.inc(last)
            in_turn(pool, NCH, place)

        @block.vector
        def _(dve):
            spline.start(dve)
            summed.start(dve)
            count = [0]

            def link(ins):
                count[0] += 1
                ins.then_inc(pre, 1)
                dve.wait_ge(pre, count[0])
            dve.wait_ge(consts, 96)
            dve.wait_ge(ext_all, 1)
            for e in range(2):
                link(dve.tensor_tensor(pr[:], oh[:], exta[:, e:e + 1, :].broadcast_to([P, TILES, NT]), ALU.mult))
                link(dve.tensor_reduce(lim[:, e, :], pr[:], AX.X, ALU.add))
            link(dve.scalar_tensor_tensor(out=diff[:], in0=lim[:, 0, :], scalar=1.0, in1=lim[:, 1, :], op0=ALU.mult, op1=ALU.add))
            link(dve.tensor_scalar(diff[:], diff[:], 1e-8, None, ALU.add))
            link(dve.reciprocal(rec[:], diff[:]))
            wide = [P, TILES, SL]
            link(dve.tensor_tensor(u[:], xs[:], lim[:, 1, :].rearrange("p (t o) -> p t o", o=1).broadcast_to(wide), ALU.add))
            link(dve.tensor_tensor(u[:], u[:], rec[:].rearrange("p (t o) -> p t o", o=1).broadcast_to(wide), ALU.mult))
            link(dve.tensor_scalar(u[:], u[:], 0.0, TOP, ALU.max, ALU.min))
            link(dve.tensor_scalar(u16[:], u[:], float(GRID), None, ALU.mult))
            flat = lambda t: t[:].rearrange("p t e -> p (t e)")
            link(dve.tensor_tensor(ge[:].rearrange("p t e g -> p (t e) g"), flat(u16).rearrange("p (t o) -> p t o", o=1).broadcast_to([P, TILES * SL, GRID + 1]),
                                   grid[:].rearrange("p (o g) -> p o g", o=1).broadcast_to([P, TILES * SL, GRID + 1]), ALU.is_ge))
            g3 = ge[:].rearrange("p t e g -> p (t e) g")
            link(dve.tensor_tensor(hot[:].rearrange("p t e g -> p (t e) g"), g3[:, :, 0:GRID], g3[:, :, 1:GRID + 1], ALU.subtract))
            link(dve.tensor_reduce(flat(gi), g3[:, :, 1:GRID], AX.X, ALU.add))
            link(dve.scalar_tensor_tensor(out=u16[:], in0=gi[:], scalar=-1.0 / GRID, in1=u[:], op0=ALU.mult, op1=ALU.add))
            link(dve.tensor_scalar(u16[:], u16[:], float(GRID), None, ALU.mult))

            def splines(c, par, half):
                spline.begin(c)
                turned.wait_all(dve, c)
                placed.wait_freed(dve, c)
                for j in range(J):
                    last = dve.tensor_tensor(wv[:, j], rows[:, par, j, 0:TW - 1].rearrange("p (k g) -> p k g", k=2),
                                             hot[:, bass.ds(c * J + j, 1)].rearrange("p o e g -> p o (e g)").broadcast_to([P, 2, SL * GRID]), ALU.mult)
                spline.link(dve, last)
                spline.link(dve, dve.tensor_reduce(bs[:].rearrange("p j k e -> p (j k e)"), wv[:].rearrange("p j k (e g) -> p (j k e) g", g=GRID), AX.X, ALU.add))
                d = delta[:, par]
                spline.link(dve, dve.tensor_tensor(d, bs[:, :, 1, :], u16[:, bass.ds(c * J, J), :], ALU.mult))
                spline.link(dve, dve.tensor_tensor(d, d, bs[:, :, 0, :], ALU.add))
                spline.inc(dve.tensor_tensor(d, d, rows[:, par, :, TW - 1:TW].broadcast_to([P, J, SL]), ALU.mult))

            def sums(c, par, half):
                summed.begin(c)
                placed.wait_all(dve, c)
                dve.wait_ge(x_in[par], (half + 1) * 16)
                summed.inc(dve.tensor_tensor(x[:, par], x[:, par], add[:, par], ALU.add))
            skewed(dve, NCH, [(1, splines), (0, sums)])

        @block.scalar
        def _(act):
            copied.start(act)
            staged.start(act)
            act.wait_ge(consts, 96)

            def copy(c, par, half):
                copied.begin(c)
                turned.wait(act, c, 1)
                copied.inc(act.copy(oht[:, par], rows[0:NT, par, :, T - P:T]))

            def stage(c, par, half):
                staged.begin(c)
                turned.wait_freed(act, c)
                hold(act, ticks_act)
                staged.inc(act.copy(ohc[:, par], oh[:, bass.ds(c * J, J), :]))
            skewed(act, NCH, [(1, stage), (0, copy)])

        @block.tensor
        def _(pe):
            turned.start(pe)
            pe.wait_ge(consts, 96)

            def look_up(c, par, half):
                turned.begin(c)
                spline.wait_freed(pe, c)
                staged.wait_all(pe, c)
                for j in range(J):
                    mm = pe.matmul(rows[0:NT, par, j, T - P:T], ohc[:, par, j, :], ident[:], start=True, stop=True)
                turned.inc(mm)
                copied.wait_all(pe, c)
                for j in range(J):
                    mm = pe.matmul(rows[:, par, j, 0:TW], oht[:, par, j, :], table[:], start=True, stop=True)
                turned.inc(mm)

            in_turn(pe, NCH, look_up)


def program(nc, x, a_log, d_col, norm_w, norm_b, x_proj, dt_proj, dt_bias, out_proj, ffn_w, ffn_b,
            ln_scale, ln_bias, wx, ww, bw, wk, wv, wr, wo, gamma, beta, slopes, table,
            ident, cluster_row, tile_row, sub_mask, head_mask, grid, out):
    B, L, D = x.shape
    N = B * L
    NCH = N // T
    Q = D // P
    scratch = lambda name, shape: nc.dram_tensor("scratch_" + name, shape, F32, kind="Internal").ap()
    by_column = [NCH, P, Q, T]
    x_rows = x.rearrange("b l d -> (b l) d")
    dt_s, v_s, z_s = (scratch(n, by_column) for n in ("dt", "v", "z"))
    y_s = scratch("y", [NCH + 1, P, Q, T])
    bc_s = scratch("bc", [NCH, P, T])
    x2_s, vv_s, x3_s = (scratch(n, [N, D]) for n in ("x2", "vv", "x3"))
    NT = table.shape[0]
    oh_s = scratch("oh", [P, N // P, NT])
    xs_s = scratch("xs", [P, N // P, D // NT])
    ext_s = scratch("ext", [P, 2, NT])
    a_s, k_s, r_s = (scratch(n, by_column) for n in ("a", "k", "r"))

    pre_phase(nc, NCH, D, x_rows, x_proj, dt_proj, norm_w, norm_b, dt_bias, ident, dt_s, v_s, z_s, bc_s)
    scan_phase(nc, B, L, a_log, d_col, ident, dt_s, v_s, z_s, bc_s, y_s)
    mid_phase(nc, NCH, D, x_rows, y_s, out_proj, ffn_w, ffn_b, ln_scale, ln_bias, wx, ww, bw, wk, wr, wv, ident, x2_s, a_s, k_s, r_s, vv_s)
    core_phase(nc, D, HEADS, L, a_s, k_s, r_s, vv_s, x2_s, wo, gamma, beta, slopes, cluster_row, tile_row, sub_mask, head_mask, ident, x3_s, oh_s, xs_s, ext_s)
    final_phase(nc, D, N, x3_s, oh_s, xs_s, ext_s, table, grid, ident, out.rearrange("b l d -> (b l) d"))


def kernel(**inputs):
    import numpy as _np
    import concourse.bacc as _bacc
    from concourse import mybir as _mybir
    from concourse.bass_utils import run_bass_kernel_spmd as _run

    f = {n: _np.asarray(a) for n, a in inputs.items()}
    rows = lambda a: _np.ascontiguousarray(a.reshape(a.shape[0] // P, P, -1).transpose(1, 0, 2))
    turned = lambda a: rows(a.T)
    column = lambda a: _np.ascontiguousarray(a.reshape(-1, P).T)
    D = f["L0_attn_x"].shape[2]
    NT = f["L1_ffn_output_scale"].shape[0]
    SL = D // NT
    p = _np.arange(P)
    const = lambda row: _np.ascontiguousarray(_np.broadcast_to(row.astype(_np.float32), (P, row.shape[-1])))
    arrays = {
        "x": f["L0_attn_x"],
        "a_log": rows(f["L0_attn_A_log"]),
        "d_col": column(f["L0_attn_D_param"]),
        "norm_w": column(f["L0_attn_norm_w"]),
        "norm_b": column(f["L0_attn_norm_b"]),
        "x_proj": turned(f["L0_attn_x_proj_w"]),
        "dt_proj": _np.ascontiguousarray(f["L0_attn_dt_proj_w"].T),
        "dt_bias": column(f["L0_attn_dt_proj_b"]),
        "out_proj": turned(f["L0_attn_out_proj_w"]),
        "ffn_w": turned(f["L0_ffn_expert_w"][0]),
        "ffn_b": f["L0_ffn_expert_b"][0],
        "ln_scale": column(f["L1_attn_ln_scale"]),
        "ln_bias": column(f["L1_attn_ln_bias"]),
        "wx": rows(f["L1_attn_Wx"]),
        "ww": turned(f["L1_attn_Ww"]),
        "bw": column(f["L1_attn_bw"]),
        "wk": turned(f["L1_attn_Wk"]),
        "wv": turned(f["L1_attn_Wv"]),
        "wr": turned(f["L1_attn_Wr"]),
        "wo": turned(f["L1_attn_Wo"]),
        "gamma": f["L1_ffn_ln_gamma"],
        "beta": f["L1_ffn_ln_beta"],
        "slopes": f["L1_ffn_spline_slopes"].reshape(-1),
        "table": _np.concatenate([f["L1_ffn_spline_bases"].reshape(NT, -1), f["L1_ffn_spline_slopes"].reshape(NT, -1),
                                  f["L1_ffn_output_scale"].reshape(NT, 1)], axis=1),
        "ident": _np.eye(P, dtype=_np.float32),
        "cluster_row": const(-2048.0 * _np.arange(NT // SL)),
        "tile_row": const(-1.0 * _np.arange(NT)),
        "sub_mask": (p[:, None] // SUB == p[None] // SUB).astype(_np.float32),
        "head_mask": (p[:, None] // (D // HEADS) == p[None] // (D // HEADS)).astype(_np.float32),
        "grid": const(_np.arange(f["L1_ffn_spline_bases"].shape[2] + 1)),
    }
    nc = _bacc.Bacc("TRN2", target_bir_lowering=False, num_devices=1)
    held, args = {}, {}
    for name, a in arrays.items():
        a = _np.ascontiguousarray(a)
        held["in_" + name] = a
        args[name] = nc.dram_tensor("in_" + name, a.shape, _mybir.dt.from_np(a.dtype), kind="ExternalInput").ap()
    args["out"] = nc.dram_tensor("out_0", f["L0_attn_x"].shape, F32, kind="ExternalOutput").ap()
    program(nc, **args)
    r = _run(nc, [held], core_ids=[0])
    return r.results[0]["out_0"]
```
